# Optimizing a Trainium2 kernel written in Bass

```python
import numpy as np
import jax
import jax.numpy as jnp

def _softmax(x, axis=-1):
    return jax.nn.softmax(x, axis=axis)

def _gelu(x):
    return jax.nn.gelu(x, approximate=True)

def _silu(x):
    return jax.nn.silu(x)

def _sigmoid(x):
    return jax.nn.sigmoid(x)

def _layernorm(x, axis=-1, eps=1e-05):
    m = jnp.mean(x, axis=axis, keepdims=True)
    v = jnp.var(x, axis=axis, keepdims=True)
    return (x - m) / jnp.sqrt(v + eps)

def _scatter_add(tgt, idx, src, axis=0):
    return tgt.at[idx].add(src)

def _segment_sum(src, seg, n):
    return jax.ops.segment_sum(src, seg, n)
kernel_name = 'mk_perceiver_d1_seqx_r2_7542b3'

def setup_inputs(seed: int=0):
    np.random.seed(seed)
    _w = jnp.asarray

    def _rec_inputs():
        import jax
        import jax.numpy as jnp
        _rk = jax.random.key(seed)
        x = -0.0002928 + 1 * jax.random.normal(jax.random.fold_in(_rk, 1), (2, 512, 512), jnp.float32)
        _lenS = 512 - jax.random.randint(jax.random.fold_in(_rk, 7), (2,), 0, max(1, 512 // 4) + 1, jnp.int32)
        _lenS2 = 8192 - jax.random.randint(jax.random.fold_in(_rk, 8), (2,), 0, max(1, 8192 // 4) + 1, jnp.int32)
        _ctx_1024P = jax.random.normal(jax.random.fold_in(_rk, 11), (2, 16, 512), jnp.float32)
        _ctx_1024c = jax.random.dirichlet(jax.random.fold_in(_rk, 511), 0.3 * jnp.ones((16,), jnp.float32), (2, 8192))
        _ctx_1024t = jnp.einsum('bsk,bkd->bsd', _ctx_1024c, _ctx_1024P)
        _ctx_1024t = _ctx_1024t * jax.lax.rsqrt(jnp.mean(jnp.square(_ctx_1024t)) + 1e-12) * 0.953939
        ctx_1024 = -1.39393e-06 + 0.999914 * (_ctx_1024t + 0.3 * jax.random.normal(jax.random.fold_in(_rk, 611), (2, 8192, 512), jnp.float32))
        return (x, ctx_1024)
    x, ctx_1024 = _rec_inputs()

    def _L0_xattn_setup():
        import jax, jax.numpy as jnp
        import numpy as np
        D_MODEL = 512
        N_HEAD = 16
        D_HEAD = D_MODEL // N_HEAD
        key = jax.random.key(seed)
        ks = jax.random.split(key, 6)
        B, L, M = (2, 1024, 1024)
        q = jax.random.normal(ks[0], (B, L, D_MODEL), dtype=jnp.float32)
        kv = jax.random.normal(ks[1], (B, L, D_MODEL), dtype=jnp.float32)
        mem = jax.random.normal(ks[2], (B, M, D_MODEL), dtype=jnp.float32)
        s = 1.0 / np.sqrt(D_MODEL)
        w_q = jax.random.normal(ks[3], (D_MODEL, D_MODEL), dtype=jnp.float32) * s
        w_kv = jax.random.normal(ks[4], (D_MODEL, 2 * D_HEAD), dtype=jnp.float32) * s
        w_concat = jax.random.normal(ks[5], (D_MODEL, D_MODEL), dtype=jnp.float32) * s
        return {'q': q, 'kv': kv, 'mem': mem, 'w_q': w_q, 'w_kv': w_kv, 'w_concat': w_concat}
    _L0_xattn_all = _L0_xattn_setup()
    _L0_xattn_in = {k: v for k, v in _L0_xattn_all.items() if k in ('w_q', 'w_kv', 'w_concat')}
    del _L0_xattn_all

    def _L0_attn_setup():
        import jax, jax.numpy as jnp
        import numpy as np
        B, N, C, H = (4, 4096, 512, 16)
        D = C // H
        key = jax.random.key(seed)
        k1, k2, k3 = jax.random.split(key, 3)
        scale_in = 1.0 / np.sqrt(C)
        return {'x': jax.random.normal(k1, (B, N, C), dtype=jnp.float32), 'w_qkv': jax.random.normal(k2, (C, 3 * C), dtype=jnp.float32) * scale_in, 'b_qkv': jnp.zeros((3 * C,), dtype=jnp.float32), 'w_proj': jax.random.normal(k3, (C, C), dtype=jnp.float32) * scale_in, 'b_proj': jnp.zeros((C,), dtype=jnp.float32)}
    _L0_attn_all = _L0_attn_setup()
    _L0_attn_in = {k: v for k, v in _L0_attn_all.items() if k in ('w_qkv', 'b_qkv', 'w_proj', 'b_proj')}
    del _L0_attn_all

    def _L0_ffn_setup():
        import jax, jax.numpy as jnp
        import numpy as np
        B, N, D, E, R, K = (4, 1024, 512, 8, 128, 2)
        key = jax.random.key(seed)
        ks = jax.random.split(key, 5)
        scale = 0.02
        return {'x': jax.random.normal(ks[0], (B, N, D), dtype=jnp.float32), 'gate_w': jax.random.normal(ks[1], (D, E), dtype=jnp.float32) * scale, 'Wu': jax.random.normal(ks[2], (E, D, R), dtype=jnp.float32) * scale, 'Wv': jax.random.normal(ks[3], (E, D, R), dtype=jnp.float32) * scale, 'Wo': jax.random.normal(ks[4], (E, R, D), dtype=jnp.float32) * scale}
    _L0_ffn_all = _L0_ffn_setup()
    _L0_ffn_in = {k: v for k, v in _L0_ffn_all.items() if k in ('gate_w', 'Wu', 'Wv', 'Wo')}
    del _L0_ffn_all
    return {'x': x, 'ctx_1024': ctx_1024, 'L0_xattn_w_q': _L0_xattn_in['w_q'], 'L0_xattn_w_kv': _L0_xattn_in['w_kv'], 'L0_xattn_w_concat': _L0_xattn_in['w_concat'], 'L0_attn_w_qkv': _L0_attn_in['w_qkv'], 'L0_attn_b_qkv': _L0_attn_in['b_qkv'], 'L0_attn_w_proj': _L0_attn_in['w_proj'], 'L0_attn_b_proj': _L0_attn_in['b_proj'], 'L0_ffn_gate_w': _L0_ffn_in['gate_w'], 'L0_ffn_Wu': _L0_ffn_in['Wu'], 'L0_ffn_Wv': _L0_ffn_in['Wv'], 'L0_ffn_Wo': _L0_ffn_in['Wo']}

def reference(x, ctx_1024, L0_xattn_w_q, L0_xattn_w_kv, L0_xattn_w_concat, L0_attn_w_qkv, L0_attn_b_qkv, L0_attn_w_proj, L0_attn_b_proj, L0_ffn_gate_w, L0_ffn_Wu, L0_ffn_Wv, L0_ffn_Wo):
    import jax
    import jax.numpy as jnp

    def _L0_xattn_ref(q, kv, mem, w_q, w_kv, w_concat):
        import jax, jax.numpy as jnp
        import numpy as np
        D_MODEL = 512
        N_HEAD = 16
        D_HEAD = D_MODEL // N_HEAD
        B, L, D = q.shape
        c = jnp.concatenate([mem, kv], axis=1)
        qh = (q @ w_q).reshape(B, L, N_HEAD, D_HEAD).transpose(0, 2, 1, 3)
        kvp = c @ w_kv
        k, v = (kvp[..., :D_HEAD], kvp[..., D_HEAD:])
        attn_score = jnp.einsum('bhid,bjd->bhij', qh, k) / np.sqrt(D_HEAD)
        attn_prob = jax.nn.softmax(attn_score, axis=-1)
        out = jnp.einsum('bhij,bjd->bhid', attn_prob, v)
        out = out.transpose(0, 2, 1, 3).reshape(B, L, D)
        return out @ w_concat

    def _L0_attn_ref(x, w_qkv, b_qkv, w_proj, b_proj):
        import jax, jax.numpy as jnp
        import numpy as np
        B, N, C, H = (4, 4096, 512, 16)
        D = C // H
        Bx, Nx, Cx = x.shape
        qkv = x @ w_qkv + b_qkv
        qkv = qkv.reshape(Bx, Nx, 3, H, D)
        qkv = jnp.transpose(qkv, (2, 0, 3, 1, 4))
        q, k, v = (qkv[0], qkv[1], qkv[2])
        q = jax.nn.elu(q) + 1.0
        k = jax.nn.elu(k) + 1.0
        kv = jnp.einsum('bhnd,bhne->bhde', k, v)
        out = jnp.einsum('bhnd,bhde->bhne', q, kv)
        z = 1.0 / (jnp.einsum('bhnd,bhd->bhn', q, k.sum(axis=2)) + 1e-08)
        out = out * z[..., None]
        out = jnp.transpose(out, (0, 2, 1, 3)).reshape(Bx, Nx, Cx)
        out = out @ w_proj + b_proj
        return out

    def _L0_ffn_ref(x, gate_w, Wu, Wv, Wo):
        import jax, jax.numpy as jnp
        import numpy as np
        B, N, D, E, R, K = (4, 1024, 512, 8, 128, 2)
        logits = jnp.einsum('bnd,de->bne', x, gate_w)
        topv, topi = jax.lax.top_k(logits, K)
        w = jax.nn.softmax(topv, axis=-1)
        u = jnp.einsum('bnd,edr->bner', x, Wu)
        v = jnp.einsum('bnd,edr->bner', x, Wv)
        s = jax.nn.silu(u) * v
        Y = jnp.einsum('bner,erd->bned', s, Wo)
        y_sel = jnp.take_along_axis(Y, topi[..., None], axis=2)
        out = jnp.einsum('bnkd,bnk->bnd', y_sel, w)
        return out
    x = x + _L0_xattn_ref(_layernorm(x, axis=-1), ctx_1024, ctx_1024, L0_xattn_w_q, L0_xattn_w_kv, L0_xattn_w_concat)
    x = x + _L0_attn_ref(_layernorm(x, axis=-1), L0_attn_w_qkv, L0_attn_b_qkv, L0_attn_w_proj, L0_attn_b_proj)
    x = x + _L0_ffn_ref(_layernorm(x, axis=-1), L0_ffn_gate_w, L0_ffn_Wu, L0_ffn_Wv, L0_ffn_Wo)
    return x

_drawn_inputs = setup_inputs


def setup_inputs(seed=0):
    import zlib

    import numpy as np

    out = dict(_drawn_inputs(seed))
    spreads = {'L0_attn_b_qkv': (0.0, 0.1), 'L0_attn_b_proj': (0.0, 0.1)}
    factors = {'L0_ffn_gate_w': 4.381, 'L0_ffn_Wu': 4.048, 'L0_ffn_Wv': 3.909, 'L0_ffn_Wo': 3.856}
    for name, (base, spread) in spreads.items():
        noise = np.random.default_rng([zlib.crc32(name.encode()), seed]).standard_normal(out[name].shape)
        drawn = base * np.exp(spread * noise) if base else spread * noise
        out[name] = jnp.asarray(drawn.astype(out[name].dtype))
    for name, factor in factors.items():
        out[name] = (out[name] * factor).astype(out[name].dtype)
    return out
```

```python
from contextlib import ExitStack

import concourse.bass as bass
from concourse import mybir

ALU = mybir.AluOpType
ACT = mybir.ActivationFunctionType
F32 = mybir.dt.float32
F16 = mybir.dt.float16
BF16 = mybir.dt.bfloat16
I32 = mybir.dt.int32
AX = mybir.AxisListType.X

P = 128
N_BANK = 512
DH = 32
SHIFT_UNIT = 64.0
EPS_LN = 1e-5
EPS_Z = 1e-8
EXPONENT_BITS = 0x7F800000


def perceiver_block(nc, x, ctx_in, w_q, w_kv, w_concat, w_qkv, b_qkv, w_proj, b_proj, gate_w, w_u, w_v, w_o, out):
    B, L, D = x.shape
    M = ctx_in.shape[1]
    H = D // DH
    E, _, R = w_u.shape
    DC = D // P
    LT = L // P
    TT = B * LT
    NG = B * M // N_BANK
    GB = NG // B
    KT = M // P
    UNITS = B * H
    STEPS = KT // 2
    NP = 4
    LEAD = 3
    SCALE = float(DH) ** -0.5
    CONSTS = 2 + 1 + 9 + E
    OC = 2 * DH + 1

    with ExitStack() as stack:
        def sb(name, shape, dt=F32):
            return stack.enter_context(nc.sbuf_tensor(name, shape, dt))

        def sem(name):
            return stack.enter_context(nc.semaphore(name))

        psum = stack.enter_context(nc.psum_tensor("psum", [P, 8, N_BANK], F32))
        resid = sb("resid", [P, TT, D])
        featT = sb("featT", [P, DC, TT * P])
        wkv_sb = sb("wkv_sb", [P, DC, 4, DH])
        ident = sb("ident", [P, P])
        blockmask = sb("blockmask", [P, P + 4])
        bn6 = sb("bn6", [P, TT, 6])
        mv = sb("mv", [P, TT, 2])
        rstd = sb("rstd", [P, TT])
        std = sb("std", [P, TT])
        kstat = sb("kstat", [P, 2, NG])
        kext = sb("kext", [P, B, 2])
        kabs = sb("kabs", [P, B])
        kpow = sb("kpow", [P, B])
        kinv = sb("kinv", [P, B])
        qpow = sb("qpow", [P, B])
        vpow = sb("vpow", [P, B])
        rowmax = sb("rowmax", [P, UNITS, LT, 4])
        shiftc = sb("shiftc", [P, UNITS * LT])
        shift_hi = sb("shift_hi", [P, P], F16)
        shift_lo = sb("shift_lo", [P, P], F16)
        warm = sb("warm", [P, 2])
        osum = sb("osum", [P, LT, OC])
        orec = sb("orec", [P, LT])
        onum = sb("onum", [P, LT, DH])

        arena = sb("arena", [P, 160 * 256])

        def region(kib, shape, dt=F32):
            n = 1
            for s in shape:
                n *= s
            size = 4 if dt == F32 else 2
            a = arena[:, int(kib * 256):int(kib * 256) + n * size // 4]
            if dt != F32:
                a = a.bitcast(dt)
            names = "abcd"[:len(shape)]
            if len(shape) == 1:
                return a
            return a.rearrange("p (%s) -> p %s" % (" ".join(names), " ".join(names)), **dict(zip(names, shape)))

        kparts = region(0, [B * M], F16)
        kvT = region(32, [B * M])
        ctx_ring = region(96, [4, 4, D])
        ctxT = region(128, [2, DC, N_BANK])
        xnorm = region(32, [TT, D])
        wq_sb = region(48, [DC, D])
        qT = region(144, [2 * DC, N_BANK])
        qparts = region(32, [UNITS, L], F16)
        prob = region(64, [NP, 2 * N_BANK])
        prob_lo = region(80, [NP, 2 * N_BANK], BF16)
        qhi = region(88, [2 * DC, N_BANK], F16)
        v_sb = region(96, [B * KT, OC], F16)
        heads = region(114, [TT, D])
        qlo = region(130, [2 * DC, N_BANK], F16)
        wc_sb = region(144, [DC, D])
        wqkv_sb = region(0, [DC, 3 * D])
        wproj_sb = region(24, [DC, D])
        wu_sb = region(32, [E, DC, R])
        wv_sb = region(48, [E, DC, R])
        wo_sb = region(64, [E, D])
        xn2 = region(144, [TT, D])
        qf = region(80, [DC, B * L])
        kf = region(96, [TT, D])
        vf = region(112, [TT, DC, P + 1])
        bias_kv = region(129, [2 * D])
        state = region(133, [B * DC, P + 4])
        ela = region(138, [2, N_BANK])
        elb = region(142, [1, N_BANK])
        la = region(144, [TT, D])
        bproj_sb = sb("bproj_sb", [P, D])
        bq_sb = sb("bq_sb", [P, DC])
        gate_sb = sb("gate_sb", [P, DC, E])
        lg = sb("lg", [P, TT, E])
        gate = sb("gate", [P, TT, E])
        gmax = sb("gmax", [P, TT])
        gsum = sb("gsum", [P, TT])
        ge = sb("ge", [P, TT, E])
        cmpa = region(112, [TT * E, E])
        cmpb = region(114, [TT * E, E])
        lower = sb("lower", [P, E, E])
        rank = sb("rank", [P, TT, E])
        zden = sb("zden", [P, 2, 2, 4])
        ffe = region(96, [2, N_BANK])
        ffr = region(100, [2, N_BANK])
        ffs = region(104, [2, N_BANK])
        fft = region(108, [2, N_BANK])

        names = """x_loaded wq_loaded wkv_loaded ctx_loaded0 ctx_loaded1 ctx_loaded2 ctx_loaded3 consts_ready
            dve_link act_link bn_done std_done xn_ready xT_tp xT_copied q_mm q_copied
            ctx_tp ctxT_copied kv_mm kv_copied stat_done kparts_ready v_scaled q_ready qparts_loaded0 qparts_loaded1 wc_loaded v_tp v_hi v_copied
            max_scores max_read shift_cols shift_tp shift_ready shift_loaded
            scores_ready exp_done lo_ready prob_slot_free out_slot_free sums_ready heads_ready
            late_loaded concat_tp concat_copied concat_mm concat_added ffnw_loaded bias_loaded
            qkv_q qkv_qexp qkv_qdone qkv_k qkv_kb qkv_kexp qkv_kdone qkv_v qkv_vdone state_mm state_done
            la_mm la_done la_tp la_copied proj_mm proj_added
            logit_mm logit_done gate_exp gate_done ffn_u ffn_v ffn_exp ffn_s ffn_y ffn_added out_done""".split()
        s = {n: sem(n) for n in names}
        x_loaded, wq_loaded, wkv_loaded, consts_ready = (s[n] for n in ("x_loaded", "wq_loaded", "wkv_loaded", "consts_ready"))
        ctx_loaded = [s[f"ctx_loaded{i}"] for i in range(4)]

        x_dram = x.rearrange("b (t p) d -> p (b t) d", p=P)
        out_dram = out.rearrange("b (t p) d -> p (b t) d", p=P)
        ctx_dram = ctx_in.rearrange("b m d -> (b m) d").rearrange("(g t p) d -> g p t d", p=P, t=4)

        block = stack.enter_context(nc.Block())

        @block.sync
        def _(sp):
            def load(dst, src, signal):
                return sp.dma_start(dst, src).then_inc(signal, 16)

            load(resid[:], x_dram, x_loaded)
            for c in range(4):
                load(ctx_ring[:, c], ctx_dram[c], ctx_loaded[c])
                if c == 0:
                    for i in range(4):
                        lo = 0 if i < 3 else DH
                        load(wkv_sb[:, :, i, :], w_kv.rearrange("(c p) n -> p c n", p=P)[:, :, lo:lo + DH], wkv_loaded)
                    load(wq_sb, w_q.rearrange("(c p) n -> p c n", p=P), wq_loaded)
            with sp.Fori(1, NG // 4) as i:
                for c in range(4):
                    sp.wait_ge(s["ctx_tp"], i * 8 + (2 * c - 6))
                    load(ctx_ring[:, c], ctx_dram[bass.ds(4 * i + c, 1)].rearrange("g p t d -> p (g t) d"), ctx_loaded[c])
            qv = qparts.rearrange("p (c j) l -> p c j l", j=4)
            for b in range(B):
                sp.wait_ge(s["q_ready"], b + 1)
                cs = slice(b * DC, (b + 1) * DC)
                for j in range(4):
                    rows = slice(DH * j, DH * (j + 1))
                    load(qv[0:DH, cs, j, :], qhi[rows, cs, :], s[f"qparts_loaded{b}"])
                    load(qv[DH:2 * DH, cs, j, :], qhi[rows, cs, :], s[f"qparts_loaded{b}"])
                    load(qv[2 * DH:3 * DH, cs, j, :], qlo[rows, cs, :], s[f"qparts_loaded{b}"])
            sp.wait_ge(s["shift_ready"], 2)
            load(qparts[3 * DH:3 * DH + 1].rearrange("p u (t q) -> p (u t) q", q=P), shift_hi[:], s["shift_loaded"])
            load(qparts[3 * DH + 1:3 * DH + 2].rearrange("p u (t q) -> p (u t) q", q=P), shift_lo[:], s["shift_loaded"])
            sp.wait_ge(s["q_ready"], B)
            load(wc_sb, w_concat.rearrange("(c p) n -> p c n", p=P), s["wc_loaded"])
            load(bproj_sb[:], b_proj.rearrange("(a n) -> a n", a=1).broadcast_to([P, D]), s["bias_loaded"])
            sp.dma_start(bq_sb[:], b_qkv[0:D].rearrange("(c p) -> p c", p=P), allow_slow_non_contiguous=True)\
                .then_inc(s["bias_loaded"], 16)
            load(gate_sb[:], gate_w.rearrange("(c p) e -> p c e", p=P), s["bias_loaded"])
            sp.wait_ge(s["heads_ready"], UNITS)
            load(wqkv_sb, w_qkv.rearrange("(c p) n -> p c n", p=P), s["late_loaded"])
            load(wproj_sb, w_proj.rearrange("(c p) n -> p c n", p=P), s["late_loaded"])
            sp.wait_ge(s["concat_tp"], TT)
            load(bias_kv, b_qkv[D:3 * D].rearrange("(a n) -> a n", a=1).broadcast_to([P, 2 * D]), s["bias_loaded"])
            for e in range(E):
                load(wu_sb[:, e], w_u[e].rearrange("(c p) r -> p c r", p=P), s["ffnw_loaded"])
                load(wv_sb[:, e], w_v[e].rearrange("(c p) r -> p c r", p=P), s["ffnw_loaded"])
            load(wo_sb, w_o.rearrange("e r d -> r e d"), s["ffnw_loaded"])
            for t in range(TT):
                sp.wait_ge(s["ffn_added"], (E - 1) * TT + t + 1)
                load(out_dram[:, t], resid[:, t], s["out_done"])
            sp.wait_ge(s["out_done"], 16 * TT)

        @block.gpsimd
        def _(pool):
            done = [0]

            def step(ins):
                done[0] += 1
                ins.then_inc(consts_ready, 1)
                pool.wait_ge(consts_ready, done[0])

            step(nc.gpsimd.memset(ident[:], 0.0))
            step(nc.gpsimd.affine_select(out=ident[:], in_=ident[:], compare_op=ALU.not_equal, fill=1.0, base=0,
                                         pattern=[[-1, P]], channel_multiplier=1))
            step(nc.gpsimd.memset(kparts[3 * DH:3 * DH + 2, :], SHIFT_UNIT))
            step(nc.gpsimd.memset(blockmask[:], 0.0))
            for j in range(4):
                rows = slice(DH * j, DH * (j + 1))
                step(nc.gpsimd.memset(blockmask[rows, DH * j:DH * (j + 1)], 1.0))
                step(nc.gpsimd.memset(blockmask[rows, P + j:P + j + 1], 1.0))
            step(nc.gpsimd.memset(lower[:], 0.0))
            for e in range(1, E):
                step(nc.gpsimd.memset(lower[:, e, 0:e], 1.0))
            assert done[0] == CONSTS

        @block.scalar
        def _(act):
            def layernorm_std(k):
                act.wait_ge(s["bn_done"], k + 1)
                nc.scalar.activation(std[:], mv[:, :, 1], ACT.Sqrt).then_inc(s["std_done"], 1)

            layernorm_std(0)
            for i in range(2 * DC):
                b, c = divmod(i, DC)
                act.wait_ge(s["xT_tp"], i + 1)
                nc.scalar.copy(featT[:, c, b * L:(b + 1) * L], psum[:, i, :]).then_inc(s["xT_copied"], 1)
            for i in range(2 * DC):
                act.wait_ge(s["q_mm"], i + 1)
                nc.scalar.copy(qT[:, i], psum[:, i, :]).then_inc(s["q_copied"], 1)
            def copy_context(c, group):
                for half in range(2):
                    act.wait_ge(s["ctx_tp"], group * 2 + (half + 1))
                    if half == 0:
                        act.wait_ge(s["kv_mm"], group + 1)
                    nc.scalar.copy(ctxT[:, c % 2, 2 * half:2 * half + 2, :],
                                   psum[:, 2 * half:2 * half + 2, :]).then_inc(s["ctxT_copied"], 1)

            def copy_keys(c, group):
                act.wait_ge(s["kv_mm"], group + 3)
                nc.scalar.copy(kvT[:, bass.ds(group * N_BANK, N_BANK)], psum[:, 4 + c % 2, :])\
                    .then_inc(s["kv_copied"], 1)

            for c in range(4):
                copy_context(c, c)
                if c:
                    copy_keys(c - 1, c - 1)
            with act.Fori(1, NG // 4) as i:
                for c in range(4):
                    copy_context(c, i * 4 + c)
                    copy_keys((c - 1) % 4, i * 4 + (c - 1))
            copy_keys(3, NG - 1)
            for i in range(B * KT // 16):
                act.wait_ge(s["v_tp"], i + 1)
                nc.scalar.copy(v_sb[:, 16 * i:16 * (i + 1), 0:DH],
                               psum[:, i % 2, :].rearrange("p (k d) -> p k d", d=DH)).then_inc(s["v_hi"], 1)
            act.wait_ge(consts_ready, CONSTS)
            nc.scalar.activation(warm[:, 0:1], ident[:, 0:1], ACT.Exp).then_inc(s["act_link"], 1)
            with act.Fori(0, UNITS * STEPS // NP) as i:
                for j in range(NP):
                    act.wait_ge(s["scores_ready"], i * NP + j + 1)
                    act.wait_ge(s["prob_slot_free"], i * NP + j + 1)
                    sl = 2 * (j % 2)
                    nc.scalar.activation(prob[:, j], psum[:, sl:sl + 2, :].rearrange("p a n -> p (a n)"),
                                         ACT.Exp, scale=SCALE).then_inc(s["exp_done"], 1)
            for i in range(TT):
                act.wait_ge(s["concat_tp"], i + 1)
                nc.scalar.activation(featT[:, :, i * P:(i + 1) * P],
                                     psum[:, i % 2, :].rearrange("p (c q) -> p c q", c=DC), ACT.Copy,
                                     scale=vpow[:, i // LT:i // LT + 1]).then_inc(s["concat_copied"], 1)
            layernorm_std(1)
            for i in range(2 * DC):
                b, c = divmod(i, DC)
                act.wait_ge(s["xT_tp"], 2 * DC + i + 1)
                nc.scalar.copy(featT[:, c, b * L:(b + 1) * L], psum[:, i, :]).then_inc(s["xT_copied"], 1)
            act.wait_ge(s["bias_loaded"], 64)
            for i in range(2 * DC):
                b, c = divmod(i, DC)
                act.wait_ge(s["qkv_q"], i + 1)
                if i >= 2:
                    act.wait_ge(s["qkv_qdone"], i - 1)
                nc.scalar.activation(ela[:, i % 2], psum[:, i % 2, :], ACT.Exp,
                                     bias=bq_sb[:, c:c + 1]).then_inc(s["qkv_qexp"], 1)
            for t in range(TT):
                act.wait_ge(s["qkv_kb"], t + 1)
                if t == 0:
                    act.wait_ge(s["qkv_qdone"], 2 * DC)
                else:
                    act.wait_ge(s["qkv_kdone"], max(t - 1, 1))
                nc.scalar.activation(ela[:, t % 2], kf[:, t], ACT.Exp).then_inc(s["qkv_kexp"], 1)
            for i in range(TT):
                act.wait_ge(s["la_tp"], i + 1)
                nc.scalar.copy(featT[:, :, i * P:(i + 1) * P],
                               psum[:, 4 + i % 2, :].rearrange("p (c q) -> p c q", c=DC)).then_inc(s["la_copied"], 1)
            layernorm_std(2)
            for i in range(2 * DC):
                b, c = divmod(i, DC)
                act.wait_ge(s["xT_tp"], 4 * DC + i + 1)
                nc.scalar.copy(featT[:, c, b * L:(b + 1) * L], psum[:, i, :]).then_inc(s["xT_copied"], 1)
            act.wait_ge(s["logit_done"], 1)
            nc.scalar.activation(ge[:], lg[:], ACT.Exp).then_inc(s["gate_exp"], 1)
            for i in range(E * B):
                act.wait_ge(s["ffn_u"], i + 1)
                if i >= 2:
                    act.wait_ge(s["ffn_s"], i - 1)
                nc.scalar.activation(ffe[:, i % 2], psum[:, i % 2, :], ACT.Exp, scale=-1.0).then_inc(s["ffn_exp"], 1)

        @block.vector
        def _(dve):
            n = [0]

            def link(ins):
                n[0] += 1
                ins.then_inc(s["dve_link"], 1)
                dve.wait_ge(s["dve_link"], n[0])

            def layernorm(k, dst):
                for t in range(TT):
                    last = nc.vector.bn_stats(bn6[:, t], resid[:, t])
                link(last)
                for t in range(TT):
                    last = nc.vector.bn_aggr(mv[:, t], bn6[:, t])
                link(last)
                nc.vector.tensor_scalar(mv[:, :, 1], mv[:, :, 1], EPS_LN, None, ALU.add).then_inc(s["bn_done"], 1)
                dve.wait_ge(s["std_done"], k + 1)
                link(nc.vector.reciprocal(rstd[:], std[:]))
                for t in range(TT):
                    nc.vector.tensor_scalar(dst[:, t], resid[:, t], mv[:, t, 0:1], rstd[:, t:t + 1],
                                            ALU.subtract, ALU.mult).then_inc(s["xn_ready"], 1)

            dve.wait_ge(x_loaded, 16)
            layernorm(0, xnorm)
            for b in range(B):
                with dve.Fori(0, GB // 4) as i:
                    for c in range(4):
                        dve.wait_ge(s["kv_copied"], (b * GB + c + 1) + i * 4)
                        src = kvT[:, bass.ds((b * GB + c) * N_BANK + i * (4 * N_BANK), N_BANK)]
                        nc.vector.tensor_reduce(kstat[:, 0, bass.ds(b * GB + c + i * 4, 1)], src, AX, ALU.max)
                        nc.vector.tensor_reduce(kstat[:, 1, bass.ds(b * GB + c + i * 4, 1)], src, AX, ALU.min)\
                            .then_inc(s["stat_done"], 1)
                dve.wait_ge(s["stat_done"], GB * (b + 1))
                gs = slice(b * GB, (b + 1) * GB)
                nc.vector.tensor_reduce(kext[:, b, 0:1], kstat[:, 0, gs], AX, ALU.max)
                link(nc.vector.tensor_reduce(kext[:, b, 1:2], kstat[:, 1, gs], AX, ALU.min))
                bb = slice(b, b + 1)
                link(nc.vector.scalar_tensor_tensor(kabs[:, bb], kext[:, b, 1:2], -1.0, kext[:, b, 0:1],
                                                    ALU.mult, ALU.max))
                link(nc.vector.tensor_scalar(kabs[:, bb], kabs[:, bb], 1e-30, None, ALU.max))
                link(nc.vector.tensor_scalar(kpow[:, bb].bitcast(I32), kabs[:, bb].bitcast(I32), EXPONENT_BITS, None,
                                             ALU.bitwise_and))
                link(nc.vector.reciprocal(kinv[:, bb], kpow[:, bb]))
                for j in range(4):
                    rows = slice(DH * j, DH * (j + 1))
                    nc.vector.tensor_copy(qpow[rows, bb], kpow[0:DH, bb])
                    last = nc.vector.tensor_copy(vpow[rows, bb], kpow[3 * DH:4 * DH, bb])
                link(last)
                keys = slice(b * M, (b + 1) * M)
                link(nc.vector.tensor_scalar(kparts[0:3 * DH, keys], kvT[0:3 * DH, keys], kinv[0:3 * DH, bb], None, ALU.mult))
                nc.vector.scalar_tensor_tensor(kparts[DH:2 * DH, keys], kvT[DH:2 * DH, keys], kinv[DH:2 * DH, bb],
                                               kparts[DH:2 * DH, keys], ALU.mult, ALU.subtract)\
                    .then_inc(s["kparts_ready"], 1)
                nc.vector.tensor_scalar(kvT[3 * DH:4 * DH, keys], kvT[3 * DH:4 * DH, keys], kinv[3 * DH:4 * DH, bb],
                                        None, ALU.mult).then_inc(s["v_scaled"], 1)
            for i in range(B * KT // 16):
                dve.wait_ge(s["v_hi"], i + 1)
                if i == 0:
                    nc.vector.memset(v_sb[:, :, 2 * DH:OC], 1.0)
                tiles = slice(16 * i, 16 * (i + 1))
                nc.vector.tensor_tensor(v_sb[:, tiles, DH:2 * DH], psum[:, i % 2, :].rearrange("p (k d) -> p k d", d=DH),
                                        v_sb[:, tiles, 0:DH], ALU.subtract).then_inc(s["v_copied"], 1)
            for b in range(B):
                cs = slice(b * DC, (b + 1) * DC)
                dve.wait_ge(s["q_copied"], DC * (b + 1))
                link(nc.vector.tensor_scalar(qhi[:, cs], qT[:, cs], qpow[:, b:b + 1], None, ALU.mult))
                nc.vector.scalar_tensor_tensor(qlo[:, cs], qT[:, cs], qpow[:, b:b + 1], qhi[:, cs],
                                               ALU.mult, ALU.subtract).then_inc(s["q_ready"], 1)
            for b in range(B):
                with dve.Fori(0, H) as h:
                    for t in range(LT):
                        for k in range(4):
                            i0 = b * H * 16 + t * 4 + k
                            dve.wait_ge(s["max_scores"], h * 16 + i0 + 1)
                            sl = 4 * (k % 2)
                            nc.vector.tensor_reduce(rowmax[:, bass.ds(h + b * H, 1), t, k:k + 1],
                                                    psum[:, sl:sl + 4, :].rearrange("p a n -> p (a n)"),
                                                    AX, ALU.max).then_inc(s["max_read"], 1)
            dve.wait_ge(s["max_read"], 2 + UNITS * 16)
            nc.vector.tensor_reduce(shiftc[:], rowmax[:].rearrange("p u t k -> p (u t) k"), AX, ALU.max)\
                .then_inc(s["shift_cols"], 1)
            dve.wait_ge(s["shift_tp"], 1)
            nc.vector.tensor_scalar(shift_hi[:], psum[:, 0, 0:P], -1.0 / SHIFT_UNIT, None, ALU.mult)\
                .then_inc(s["shift_ready"], 1)
            dve.wait_ge(s["shift_ready"], 1)
            nc.vector.scalar_tensor_tensor(shift_lo[:], psum[:, 0, 0:P], -1.0 / SHIFT_UNIT, shift_hi[:],
                                           ALU.mult, ALU.subtract).then_inc(s["shift_ready"], 1)

            def split_round(step0):
                for j in range(NP):
                    dve.wait_ge(s["exp_done"], step0 + (j + 3))
                    hi = prob[:, j].bitcast(BF16).rearrange("p (n two) -> p n two", two=2)[:, :, 1]
                    nc.vector.tensor_tensor(prob_lo[:, j], prob[:, j], hi, ALU.subtract).then_inc(s["lo_ready"], 1)

            def finish_unit(u, b, h, slot):
                dve.wait_ge(s["prob_slot_free"], u * STEPS + (STEPS + NP))
                o = psum[:, 4 + slot, 0:LT * OC].rearrange("p (t c) -> p t c", c=OC)
                nc.vector.tensor_copy(osum[:], o).then_inc(s["out_slot_free"], 1)
                dve.wait_ge(s["out_slot_free"], u + 3)
                nc.vector.reciprocal(orec[:], osum[:, :, 2 * DH]).then_inc(s["sums_ready"], 1)
                nc.vector.tensor_tensor(onum[:], osum[:, :, 0:DH], osum[:, :, DH:2 * DH], ALU.add)\
                    .then_inc(s["sums_ready"], 1)
                dve.wait_ge(s["sums_ready"], u * 2 + 2)
                dst = heads[:, b * LT:(b + 1) * LT, bass.ds(h * DH, DH)]
                nc.vector.tensor_tensor(dst, onum[:], orec[:].rearrange("p (t a) -> p t a", a=1).broadcast_to([P, LT, DH]),
                                        ALU.mult).then_inc(s["heads_ready"], 1)

            def split_unit(u, before=None):
                split_round(u * STEPS)
                if before is not None:
                    finish_unit(*before)
                with dve.Fori(1, STEPS // NP) as i:
                    split_round(i * NP + u * STEPS)

            for b in range(B):
                u0 = b * H
                split_unit(u0, None if b == 0 else (u0 - 1, b - 1, H - 1, 1))
                split_unit(u0 + 1, (u0, b, 0, 0))
                with dve.Fori(1, H // 2) as pair:
                    split_unit(pair * 2 + u0, (pair * 2 + (u0 - 1), b, pair * 2 - 1, 1))
                    split_unit(pair * 2 + (u0 + 1), (pair * 2 + u0, b, pair * 2, 0))
            finish_unit(UNITS - 1, B - 1, H - 1, 1)
            dve.wait_ge(s["heads_ready"], UNITS)

            for t in range(TT):
                dve.wait_ge(s["concat_mm"], t + 1)
                nc.vector.tensor_tensor(resid[:, t], psum[:, 2 + t % 2, :], resid[:, t], ALU.add)\
                    .then_inc(s["concat_added"], 1)
            dve.wait_ge(s["concat_added"], TT)
            layernorm(1, xn2)
            dve.wait_ge(s["bias_loaded"], 64)
            for i in range(2 * DC):
                b, c = divmod(i, DC)
                dve.wait_ge(s["qkv_qexp"], i + 1)
                link(nc.vector.tensor_scalar(elb[:, 0], psum[:, i % 2, :], bq_sb[:, c:c + 1], 0.0, ALU.add, ALU.max))
                nc.vector.scalar_tensor_tensor(qf[:, c, b * L:(b + 1) * L], ela[:, i % 2], 1.0, elb[:, 0],
                                               ALU.min, ALU.add).then_inc(s["qkv_qdone"], 1)
                dve.wait_ge(s["qkv_qdone"], i + 1)
            link(nc.vector.memset(vf[:, :, :, P:P + 1], 1.0))
            for t in range(TT):
                dve.wait_ge(s["qkv_k"], t + 1)
                nc.vector.tensor_tensor(kf[:, t], psum[:, 2 + t % 2, :], bias_kv[:, 0:D], ALU.add).then_inc(s["qkv_kb"], 1)
                dve.wait_ge(s["qkv_v"], t + 1)
                nc.vector.tensor_tensor(vf[:, t, :, 0:P], psum[:, 4 + t % 2, :].rearrange("p (c n) -> p c n", c=DC),
                                        bias_kv[:, D:2 * D].rearrange("p (c n) -> p c n", c=DC), ALU.add)\
                    .then_inc(s["qkv_vdone"], 1)
                dve.wait_ge(s["qkv_kexp"], t + 1)
                link(nc.vector.tensor_scalar(kf[:, t], kf[:, t], 0.0, None, ALU.max))
                nc.vector.scalar_tensor_tensor(kf[:, t], ela[:, t % 2], 1.0, kf[:, t], ALU.min, ALU.add)\
                    .then_inc(s["qkv_kdone"], 1)
            for i in range(2 * DC):
                dve.wait_ge(s["state_mm"], i + 1)
                ps = psum[:, i % 2, :]
                nc.vector.tensor_tensor(state[:, i, 0:P], ps[:, 0:P], blockmask[:, 0:P], ALU.mult)
                nc.vector.tensor_scalar(state[:, i, P:P + 4], blockmask[:, P:P + 4], ps[:, P:P + 1], None, ALU.mult)\
                    .then_inc(s["state_done"], 1)
            for t in range(TT):
                dve.wait_ge(s["la_mm"], t + 1)
                sl = 2 * (t % 2)
                o = psum[:, sl:sl + 2, 0:2 * (P + 4)].rearrange("p a (c n) -> p a c n", c=2)
                link(nc.vector.tensor_scalar(zden[:], o[:, :, :, P:P + 4], EPS_Z, None, ALU.add))
                link(nc.vector.reciprocal(zden[:], zden[:]))
                for a in range(2):
                    last = nc.vector.tensor_tensor(
                        la[:, t, a * 256:(a + 1) * 256].rearrange("p (c j d) -> p c j d", c=2, j=4),
                        o[:, a, :, 0:P].rearrange("p c (j d) -> p c j d", j=4),
                        zden[:, a].rearrange("p c (j o) -> p c j o", o=1).broadcast_to([P, 2, 4, DH]), ALU.mult)
                last.then_inc(s["la_done"], 1)
                dve.wait_ge(s["la_done"], t + 1)
            for t in range(TT):
                nc.vector.tensor_tensor(resid[:, t], resid[:, t], bproj_sb[:], ALU.add).then_inc(s["dve_link"], 1)
                n[0] += 1
            dve.wait_ge(s["dve_link"], n[0])
            for t in range(TT):
                dve.wait_ge(s["proj_mm"], t + 1)
                nc.vector.tensor_tensor(resid[:, t], psum[:, 6 + t % 2, :], resid[:, t], ALU.add)\
                    .then_inc(s["proj_added"], 1)
            dve.wait_ge(s["proj_added"], TT)
            layernorm(2, xn2)
            dve.wait_ge(consts_ready, CONSTS)
            dve.wait_ge(s["logit_mm"], 1)
            link(nc.vector.tensor_copy(lg[:], psum[:, 7, 0:TT * E].rearrange("p (t e) -> p t e", e=E)))
            flat = lg[:].rearrange("p t e -> p (t e)")
            for e in range(E):
                le = lg[:, :, e:e + 1].broadcast_to([P, TT, E])
                ca = cmpa.rearrange("p (t e) j -> p t e j", e=E)[:, :, e, :]
                cb = cmpb.rearrange("p (t e) j -> p t e j", e=E)[:, :, e, :]
                nc.vector.tensor_tensor(ca, lg[:], le, ALU.is_gt)
                link(nc.vector.tensor_tensor(cb, lg[:], le, ALU.is_equal))
                link(nc.vector.tensor_tensor(cb, cb, lower[:, e:e + 1, :].broadcast_to([P, TT, E]), ALU.mult))
            link(nc.vector.tensor_tensor(cmpa, cmpa, cmpb, ALU.add))
            link(nc.vector.tensor_reduce(rank[:].rearrange("p t e -> p (t e)"), cmpa, AX, ALU.add))
            link(nc.vector.tensor_scalar(rank[:], rank[:], 1.5, None, ALU.is_lt))
            link(nc.vector.tensor_reduce(gmax[:], lg[:], AX, ALU.max))
            nc.vector.tensor_tensor(lg[:], lg[:], gmax[:].rearrange("p (t o) -> p t o", o=1).broadcast_to([P, TT, E]),
                                    ALU.subtract).then_inc(s["logit_done"], 1)
            dve.wait_ge(s["gate_exp"], 1)
            link(nc.vector.tensor_tensor(gate[:], ge[:], rank[:], ALU.mult))
            link(nc.vector.tensor_reduce(gsum[:], gate[:], AX, ALU.add))
            link(nc.vector.reciprocal(gsum[:], gsum[:]))
            link(nc.vector.tensor_tensor(gate[:], gate[:],
                                         gsum[:].rearrange("p (t o) -> p t o", o=1).broadcast_to([P, TT, E]), ALU.mult))

            def add_experts(i):
                e, b = divmod(i, B)
                for t in range(LT):
                    k = i * LT + t
                    dve.wait_ge(s["ffn_y"], k + 1)
                    tok = b * LT + t
                    if e:
                        dve.wait_ge(s["ffn_added"], k - B * LT + 1)
                    nc.vector.scalar_tensor_tensor(resid[:, tok], psum[:, 4 + k % 4, :], gate[:, tok, e:e + 1],
                                                   resid[:, tok], ALU.mult, ALU.add).then_inc(s["ffn_added"], 1)

            for i in range(E * B):
                dve.wait_ge(s["ffn_exp"], i + 1)
                link(nc.vector.tensor_scalar(ffe[:, i % 2], ffe[:, i % 2], 1.0, None, ALU.add))
                link(nc.vector.reciprocal(ffr[:, i % 2], ffe[:, i % 2]))
                link(nc.vector.tensor_tensor(fft[:, i % 2], psum[:, i % 2, :], ffr[:, i % 2], ALU.mult))
                dve.wait_ge(s["ffn_v"], i + 1)
                nc.vector.tensor_tensor(ffs[:, i % 2], psum[:, 2 + i % 2, :], fft[:, i % 2], ALU.mult)\
                    .then_inc(s["ffn_s"], 1)
                if i >= 1:
                    add_experts(i - 1)
            add_experts(E * B - 1)

        @block.tensor
        def _(pe):
            def transpose_tokens(k, src):
                for i in range(2 * DC):
                    b, c = divmod(i, DC)
                    if c == 0:
                        pe.wait_ge(s["xn_ready"], k * TT + (b + 1) * LT)
                    for t in range(LT):
                        last = nc.tensor.transpose(psum[:, i, t * P:(t + 1) * P],
                                                   src[:, b * LT + t, c * P:(c + 1) * P], ident[:])
                    last.then_inc(s["xT_tp"], 1)

            pe.wait_ge(consts_ready, 2)
            transpose_tokens(0, xnorm)
            pe.wait_ge(wq_loaded, 16)
            pe.wait_ge(s["xT_copied"], 2 * DC)
            for i in range(2 * DC):
                b, m = divmod(i, DC)
                for c in range(DC):
                    last = nc.tensor.matmul(psum[:, i, :], wq_sb[:, c, m * P:(m + 1) * P],
                                            featT[:, c, b * L:(b + 1) * L], start=(c == 0), stop=(c == DC - 1))
                last.then_inc(s["q_mm"], 1)
            pe.wait_ge(s["q_copied"], 2 * DC)
            pe.wait_ge(wkv_loaded, 64)
            pe.sem_inc(s["kv_mm"], 2)

            def transpose_context(c, loaded, copied):
                pe.wait_ge(ctx_loaded[c], loaded)
                for half in range(2):
                    if copied is not None:
                        pe.wait_ge(s["ctxT_copied"], copied + half)
                    for cc in range(2):
                        for t in range(4):
                            f = 2 * half + cc
                            last = nc.tensor.transpose(psum[:, f, t * P:(t + 1) * P],
                                                       ctx_ring[:, c, t, f * P:(f + 1) * P], ident[:])
                    last.then_inc(s["ctx_tp"], 1)

            def multiply_context(c, copied, free):
                pe.wait_ge(s["ctxT_copied"], copied)
                if free is not None:
                    pe.wait_ge(s["kv_copied"], free)
                for f in range(DC):
                    last = nc.tensor.matmul(psum[:, 4 + c % 2, :], wkv_sb[:, f].rearrange("p a n -> p (a n)"),
                                            ctxT[:, c % 2, f, :], start=(f == 0), stop=(f == DC - 1))
                last.then_inc(s["kv_mm"], 1)

            transpose_context(0, 16, None)
            for c in range(4):
                if c < 3:
                    transpose_context(c + 1, 16, 2 * c + 1)
                else:
                    transpose_context(0, 32, 2 * c + 1)
                multiply_context(c, 2 * c + 2, c - 1 if c >= 2 else None)
            with pe.Fori(1, NG // 4 - 1) as i:
                for c in range(4):
                    if c < 3:
                        transpose_context(c + 1, i * 16 + 16, i * 8 + 2 * c + 1)
                    else:
                        transpose_context(0, i * 16 + 32, i * 8 + 2 * c + 1)
                    multiply_context(c, i * 8 + 2 * c + 2, i * 4 + c - 1)
            last_round = NG // 4 - 1
            for c in range(4):
                if c < 3:
                    transpose_context(c + 1, last_round * 16 + 16, last_round * 8 + 2 * c + 1)
                multiply_context(c, last_round * 8 + 2 * c + 2, last_round * 4 + c - 1)

            for i in range(B * KT // 16):
                if i % (KT // 16) == 0:
                    pe.wait_ge(s["v_scaled"], i // (KT // 16) + 1)
                if i >= 2:
                    pe.wait_ge(s["v_copied"], i - 1)
                else:
                    pe.wait_ge(s["ctxT_copied"], 2 * NG)
                for k in range(16):
                    last = nc.tensor.transpose(psum[:, i % 2, k * DH:(k + 1) * DH],
                                               kvT[3 * DH:4 * DH, (16 * i + k) * P:(16 * i + k + 1) * P],
                                               ident[3 * DH:4 * DH, 3 * DH:4 * DH])
                last.then_inc(s["v_tp"], 1)

            pe.wait_ge(s["kparts_ready"], B)
            pe.wait_ge(s["v_copied"], B * KT // 16)
            pe.wait_ge(s["kv_copied"], NG)
            pe.sem_inc(s["max_read"], 2)
            for b in range(B):
                pe.wait_ge(s[f"qparts_loaded{b}"], 16 * 12)
                with pe.Fori(0, H) as h:
                    for t in range(LT):
                        for k in range(4):
                            pe.wait_ge(s["max_read"], h * 16 + (b * H * 16 + t * 4 + k + 1))
                            for a in range(4):
                                lhs = qparts[0:3 * DH, bass.ds(h + b * H, 1), t * P:(t + 1) * P]
                                last = nc.tensor.matmul(psum[:, 4 * (k % 2) + a, :], lhs.rearrange("p u q -> p (u q)"),
                                                        kparts[0:3 * DH, b * M + (4 * k + a) * N_BANK:
                                                               b * M + (4 * k + a + 1) * N_BANK], start=True, stop=True)
                            last.then_inc(s["max_scores"], 1)
            pe.wait_ge(s["shift_cols"], 1)
            nc.tensor.transpose(psum[:, 0, 0:P], shiftc[:], ident[:]).then_inc(s["shift_tp"], 1)
            pe.wait_ge(s["shift_ready"], 2)
            pe.wait_ge(s["shift_loaded"], 32)

            pe.sem_inc(s["exp_done"], 2)
            pe.sem_inc(s["prob_slot_free"], NP)
            pe.sem_inc(s["out_slot_free"], 2)

            def scores(b, h, step, j, count):
                pe.wait_ge(s["exp_done"], count)
                q = qparts[0:3 * DH + 2, bass.ds(h + b * H, 1), :].rearrange("p u q -> p (u q)")
                for a in range(2):
                    keys = kparts[0:3 * DH + 2, bass.ds(step * (2 * P) + (b * M + a * P), P)]
                    last = nc.tensor.matmul(psum[:, 2 * (j % 2) + a, :], keys, q, start=True, stop=True)
                last.then_inc(s["scores_ready"], 1)

            def values(b, step, j, done, slot, first, last_step):
                pe.wait_ge(s["lo_ready"], done)
                hi = prob[:, j].bitcast(BF16).rearrange("p (n two) -> p n two", two=2)[:, :, 1]
                for a in range(2):
                    v = v_sb[:, bass.ds(step * 2 + (b * KT + a), 1), :].rearrange("p k c -> p (k c)")
                    for t in range(LT):
                        q = slice(a * N_BANK + t * P, a * N_BANK + (t + 1) * P)
                        for part, lhs in enumerate((hi[:, q], prob_lo[:, j, q])):
                            mm = nc.tensor.matmul(psum[:, 4 + slot, t * OC:(t + 1) * OC], lhs, v,
                                                  start=(first and a == 0 and t == 0 and part == 0),
                                                  stop=(last_step and a == 1 and part == 1), skip_group_check=True)
                mm.then_inc(s["prob_slot_free"], 1)

            def unit(b, h, slot, nxt):
                u = h + b * H
                pe.wait_ge(s["out_slot_free"], u + 1)

                def round_of_steps(i, first, last_round):
                    for j in range(NP):
                        step = i * NP + j
                        count = u * STEPS + step
                        if not (last_round and j >= NP - LEAD):
                            scores(b, h, step + LEAD, j + LEAD, count + (LEAD + 1))
                        elif nxt is not None:
                            scores(nxt[0], nxt[1], j - (NP - LEAD), j + LEAD, count + (LEAD + 1))
                        values(b, step, j, count + 1, slot, first and j == 0, last_round and j == NP - 1)

                round_of_steps(0, True, False)
                with pe.Fori(1, STEPS // NP - 1) as i:
                    round_of_steps(i, False, False)
                round_of_steps(STEPS // NP - 1, False, True)

            pe.wait_ge(consts_ready, CONSTS)
            for j in range(LEAD):
                scores(0, 0, j, j, j + 1)
            for b in range(B):
                with pe.Fori(0, H // 2 - 1) as pair:
                    unit(b, pair * 2, 0, (b, pair * 2 + 1))
                    unit(b, pair * 2 + 1, 1, (b, pair * 2 + 2))
                unit(b, H - 2, 0, (b, H - 1))
                unit(b, H - 1, 1, (b + 1, 0) if b + 1 < B else None)

            pe.wait_ge(s["heads_ready"], UNITS)
            pe.wait_ge(s["wc_loaded"], 16)

            def token_products(src_rows, dst, weights, cols, signal):
                for c in range(DC):
                    last = nc.tensor.matmul(dst, featT[:, c, src_rows], weights[:, c, cols],
                                            start=(c == 0), stop=(c == DC - 1))
                last.then_inc(signal, 1)

            def concat(t):
                pe.wait_ge(s["concat_copied"], t + 1)
                if t >= 2:
                    pe.wait_ge(s["concat_added"], t - 1)
                token_products(slice(t * P, (t + 1) * P), psum[:, 2 + t % 2, :], wc_sb, slice(0, D), s["concat_mm"])

            for t in range(TT):
                if t >= 2:
                    pe.wait_ge(s["concat_copied"], t - 1)
                for c in range(DC):
                    last = nc.tensor.transpose(psum[:, t % 2, c * P:(c + 1) * P], heads[:, t, c * P:(c + 1) * P], ident[:])
                last.then_inc(s["concat_tp"], 1)
                if t:
                    concat(t - 1)
            concat(TT - 1)

            transpose_tokens(1, xn2)
            pe.wait_ge(s["late_loaded"], 32)
            pe.wait_ge(s["xT_copied"], 4 * DC)
            for i in range(2 * DC):
                b, m = divmod(i, DC)
                if i >= 2:
                    pe.wait_ge(s["qkv_qdone"], i - 1)
                for c in range(DC):
                    last = nc.tensor.matmul(psum[:, i % 2, :], wqkv_sb[:, c, m * P:(m + 1) * P],
                                            featT[:, c, b * L:(b + 1) * L], start=(c == 0), stop=(c == DC - 1))
                last.then_inc(s["qkv_q"], 1)
            for t in range(TT):
                rows = slice(t * P, (t + 1) * P)
                if t >= 2:
                    pe.wait_ge(s["qkv_kb"], t - 1)
                token_products(rows, psum[:, 2 + t % 2, :], wqkv_sb, slice(D, 2 * D), s["qkv_k"])
                if t >= 2:
                    pe.wait_ge(s["qkv_vdone"], t - 1)
                token_products(rows, psum[:, 4 + t % 2, :], wqkv_sb, slice(2 * D, 3 * D), s["qkv_v"])
            pe.wait_ge(s["qkv_qdone"], 2 * DC)
            for i in range(2 * DC):
                b, c = divmod(i, DC)
                pe.wait_ge(s["qkv_kdone"], (b + 1) * LT)
                pe.wait_ge(s["qkv_vdone"], (b + 1) * LT)
                if i >= 2:
                    pe.wait_ge(s["state_done"], i - 1)
                for t in range(LT):
                    last = nc.tensor.matmul(psum[:, i % 2, 0:P + 1], kf[:, b * LT + t, c * P:(c + 1) * P],
                                            vf[:, b * LT + t, c, :], start=(t == 0), stop=(t == LT - 1))
                last.then_inc(s["state_mm"], 1)
            pe.wait_ge(s["state_done"], 2 * DC)
            for t in range(TT):
                if t >= 2:
                    pe.wait_ge(s["la_done"], t - 1)
                for c in range(DC):
                    last = nc.tensor.matmul(psum[:, 2 * (t % 2) + c // 2, (c % 2) * (P + 4):(c % 2 + 1) * (P + 4)],
                                            qf[:, c, t * P:(t + 1) * P], state[:, (t // LT) * DC + c, :],
                                            start=True, stop=True)
                last.then_inc(s["la_mm"], 1)

            def project(t):
                pe.wait_ge(s["la_copied"], t + 1)
                if t >= 2:
                    pe.wait_ge(s["proj_added"], t - 1)
                token_products(slice(t * P, (t + 1) * P), psum[:, 6 + t % 2, :], wproj_sb, slice(0, D), s["proj_mm"])

            for t in range(TT):
                pe.wait_ge(s["la_done"], t + 1)
                if t >= 2:
                    pe.wait_ge(s["la_copied"], t - 1)
                for c in range(DC):
                    last = nc.tensor.transpose(psum[:, 4 + t % 2, c * P:(c + 1) * P], la[:, t, c * P:(c + 1) * P], ident[:])
                last.then_inc(s["la_tp"], 1)
                if t:
                    project(t - 1)
            project(TT - 1)

            transpose_tokens(2, xn2)
            pe.wait_ge(s["xT_copied"], 6 * DC)
            for t in range(TT):
                for c in range(DC):
                    last = nc.tensor.matmul(psum[:, 7, t * E:(t + 1) * E], featT[:, c, t * P:(t + 1) * P],
                                            gate_sb[:, c, :], start=(c == 0), stop=(c == DC - 1))
            last.then_inc(s["logit_mm"], 1)
            pe.wait_ge(s["ffnw_loaded"], 16 * (2 * E + 1))
            pe.wait_ge(s["logit_done"], 1)

            def expert_out(i):
                e, b = divmod(i, B)
                pe.wait_ge(s["ffn_s"], i + 1)
                for t in range(LT):
                    k = i * LT + t
                    if k >= 4:
                        pe.wait_ge(s["ffn_added"], k - 3)
                    nc.tensor.matmul(psum[:, 4 + k % 4, :], ffs[:, i % 2, t * P:(t + 1) * P], wo_sb[:, e, :],
                                     start=True, stop=True).then_inc(s["ffn_y"], 1)

            for i in range(E * B):
                e, b = divmod(i, B)
                if i >= 2:
                    pe.wait_ge(s["ffn_s"], i - 1)
                for bank, weights, signal in ((0, wu_sb, s["ffn_u"]), (2, wv_sb, s["ffn_v"])):
                    for c in range(DC):
                        last = nc.tensor.matmul(psum[:, bank + i % 2, :], weights[:, e, c, :],
                                                featT[:, c, b * L:(b + 1) * L], start=(c == 0), stop=(c == DC - 1))
                    last.then_inc(signal, 1)
                if i:
                    expert_out(i - 1)
            expert_out(E * B - 1)


_INS = ['x', 'ctx_1024', 'L0_xattn_w_q', 'L0_xattn_w_kv', 'L0_xattn_w_concat', 'L0_attn_w_qkv', 'L0_attn_b_qkv',
        'L0_attn_w_proj', 'L0_attn_b_proj', 'L0_ffn_gate_w', 'L0_ffn_Wu', 'L0_ffn_Wv', 'L0_ffn_Wo']
_OUTS = [((2, 512, 512), 'float32')]


def kernel(**inputs):
    import numpy as _np
    import concourse.bacc as _bacc
    from concourse import mybir as _mybir
    from concourse.bass_utils import run_bass_kernel_spmd as _run

    nc = _bacc.Bacc("TRN2", target_bir_lowering=False, num_devices=1)
    arrays, args = {}, []
    for name in _INS:
        a = _np.ascontiguousarray(inputs[name])
        arrays[f"in_{name}_dram"] = a
        args.append(nc.dram_tensor(f"in_{name}_dram", a.shape, _mybir.dt.from_np(a.dtype), kind="ExternalInput").ap())
    for i, (shape, dtype) in enumerate(_OUTS):
        dt = _mybir.dt.from_np(_np.dtype(dtype))
        args.append(nc.dram_tensor(f"out_{i}_dram", shape, dt, kind="ExternalOutput").ap())
    perceiver_block(nc, *args)
    r = _run(nc, [arrays], core_ids=[0])
    got = tuple(r.results[0][f"out_{i}_dram"] for i in range(len(_OUTS)))
    return got[0]
```

```python
from contextlib import ExitStack

import concourse.bass as bass
from concourse import mybir

ALU = mybir.AluOpType
ACT = mybir.ActivationFunctionType
F32 = mybir.dt.float32
F16 = mybir.dt.float16
BF16 = mybir.dt.bfloat16
I32 = mybir.dt.int32
AX = mybir.AxisListType.X

P = 128
N_BANK = 512
DH = 32
SHIFT_UNIT = 64.0
EPS_LN = 1e-5
EPS_Z = 1e-8
EXPONENT_BITS = 0x7F800000
GAP_LIMIT = 60.0


def perceiver_block(nc, x, ctx_in, w_q, w_kv, w_concat, w_qkv, b_qkv, w_proj, b_proj, gate_w, w_u, w_v, w_o, out):
    B, L, D = x.shape
    M = ctx_in.shape[1]
    H = D // DH
    E, _, R = w_u.shape
    DC = D // P
    LT = L // P
    TT = B * LT
    NG = B * M // N_BANK
    GB = NG // B
    KT = M // P
    UNITS = B * H
    STEPS = KT // 2
    NP = 8
    LEAD = 5
    SCALE = float(DH) ** -0.5
    CONSTS = 2 + 4 + 9 + E
    OC = 2 * DH + 1

    with ExitStack() as stack:
        def sb(name, shape, dt=F32):
            return stack.enter_context(nc.sbuf_tensor(name, shape, dt))

        def sem(name):
            return stack.enter_context(nc.semaphore(name))

        psum = stack.enter_context(nc.psum_tensor("psum", [P, 8, N_BANK], F32))
        resid = sb("resid", [P, TT, D])
        featT = sb("featT", [P, DC, TT * P])
        wkv_sb = sb("wkv_sb", [P, DC, 4, DH])
        ident = sb("ident", [P, P])
        blockmask = sb("blockmask", [P, P + 4])
        bn6 = sb("bn6", [P, TT, 6])
        mv = sb("mv", [P, TT, 2])
        rstd = sb("rstd", [P, TT])
        std = sb("std", [P, TT])
        kstat = sb("kstat", [P, 3, NG])
        kext = sb("kext", [P, B, 3])
        kbox = sb("kbox", [P, B, 4])
        kbox4 = sb("kbox4", [P, B, 4])
        boxw = sb("boxw", [P, B, 2, DH + 4])
        gap = sb("gap", [P, B])
        gap_ok = sb("gap_ok", [P, 2])
        go_general = sb("go_general", [P, 2], I32)
        kabs = sb("kabs", [P, B])
        kpow = sb("kpow", [P, B])
        kinv = sb("kinv", [P, B])
        qpow = sb("qpow", [P, B])
        vpow = sb("vpow", [P, B])
        rowmax = sb("rowmax", [P, UNITS, LT, 4])
        ones = sb("ones", [P, 2])
        shiftc = sb("shiftc", [P, UNITS * LT])
        shift_hi = sb("shift_hi", [P, P], F16)
        shift_lo = sb("shift_lo", [P, P], F16)
        warm = sb("warm", [P, 2])
        zeros = sb("zeros", [DH, P], F16)

        arena = sb("arena", [P, 160 * 256])

        def region(kib, shape, dt=F32):
            n = 1
            for s in shape:
                n *= s
            size = 4 if dt == F32 else 2
            a = arena[:, int(kib * 256):int(kib * 256) + n * size // 4]
            if dt != F32:
                a = a.bitcast(dt)
            names = "abcd"[:len(shape)]
            if len(shape) == 1:
                return a
            return a.rearrange("p (%s) -> p %s" % (" ".join(names), " ".join(names)), **dict(zip(names, shape)))

        kparts = region(0, [B * M], F16)
        kvT = region(32, [B * M])
        ctx_ring = region(96, [4, 4, D])
        ctxT = region(128, [2, DC, N_BANK])
        xnorm = region(32, [TT, D])
        wq_sb = region(48, [DC, D])
        qT = region(144, [2 * DC, N_BANK])
        qparts = region(32, [UNITS, L], F16)
        prob = region(64, [NP, 2 * N_BANK])
        prob_lo = featT[:].rearrange("p c n -> p (c n)").bitcast(BF16).rearrange("p (a n) -> p a n", a=NP)
        qhi = region(88, [2 * DC, N_BANK], F16)
        v_sb = region(96, [B * KT, OC], F16)
        sums = region(112.25, [UNITS, LT, OC])
        sum_rec = region(96, [UNITS, LT])
        heads = region(64, [TT, D])
        qlo = region(130, [2 * DC, N_BANK], F16)
        wc_sb = region(146, [DC, D])
        qpos = region(64, [DC, N_BANK])
        qneg = region(72, [DC, N_BANK])
        box_hi = region(80, [2 * DC, N_BANK], F16)
        box_lo = region(152, [2 * DC, N_BANK], F16)
        wqkv_sb = region(0, [DC, 3 * D])
        wproj_sb = region(24, [DC, D])
        wu_sb = region(32, [E, DC, R])
        wv_sb = region(48, [E, DC, R])
        wo_sb = region(64, [E, D])
        xn2 = region(144, [TT, D])
        qf = region(80, [DC, B * L])
        kf = region(96, [TT, D])
        vf = region(112, [TT, DC, P + 1])
        bias_kv = region(129, [2 * D])
        state = region(133, [B * DC, P + 4])
        ela = region(138, [2, N_BANK])
        elb = region(142, [1, N_BANK])
        la = region(144, [TT, D])
        bproj_sb = sb("bproj_sb", [P, D])
        bq_sb = sb("bq_sb", [P, DC])
        gate_sb = sb("gate_sb", [P, DC, E])
        lg = sb("lg", [P, TT, E])
        gate = sb("gate", [P, TT, E])
        gmax = sb("gmax", [P, TT])
        gsum = sb("gsum", [P, TT])
        ge = sb("ge", [P, TT, E])
        cmpa = region(112, [TT * E, E])
        cmpb = region(114, [TT * E, E])
        lower = sb("lower", [P, E, E])
        rank = sb("rank", [P, TT, E])
        zden = sb("zden", [P, 2, 2, 4])
        ffe = region(96, [2, N_BANK])
        ffr = region(100, [2, N_BANK])
        ffs = region(104, [2, N_BANK])
        fft = region(108, [2, N_BANK])

        names = """x_loaded wq_loaded wkv_loaded ctx_loaded0 ctx_loaded1 ctx_loaded2 ctx_loaded3 consts_ready
            dve_link act_link bn_done std_done xn_ready xT_tp xT_copied q_mm q_copied
            ctx_tp ctxT_copied kv_mm kv_copied stat_done kparts_ready v_scaled q_ready qparts_loaded0 qparts_loaded1 wc_loaded v_tp v_hi v_copied
            max_scores max_read shift_cols shift_tp shift_ready shift_loaded shift_final qneg_ready qsplit box_mm box_hi_ready box_ready box_loaded gap_ready gap_count flag_ready
            scores_ready exp_done lo_ready prob_slot_free out_slot_free heads_ready sums_done
            late_loaded concat_tp concat_copied concat_mm concat_added ffnw_loaded bias_loaded
            qkv_q qkv_qexp qkv_qdone qkv_k qkv_kb qkv_kexp qkv_kdone qkv_v qkv_vdone state_mm state_done
            la_mm la_done la_tp la_copied proj_mm proj_added
            logit_mm logit_done gate_exp gate_done ffn_u ffn_v ffn_exp ffn_s ffn_y ffn_added out_done""".split()
        s = {n: sem(n) for n in names}
        x_loaded, wq_loaded, wkv_loaded, consts_ready = (s[n] for n in ("x_loaded", "wq_loaded", "wkv_loaded", "consts_ready"))
        ctx_loaded = [s[f"ctx_loaded{i}"] for i in range(4)]

        x_dram = x.rearrange("b (t p) d -> p (b t) d", p=P)
        out_dram = out.rearrange("b (t p) d -> p (b t) d", p=P)
        ctx_dram = ctx_in.rearrange("b m d -> (b m) d").rearrange("(g t p) d -> g p t d", p=P, t=4)

        block = stack.enter_context(nc.Block())

        @block.sync
        def _(sp):
            def load(dst, src, signal):
                return sp.dma_start(dst, src).then_inc(signal, 16)

            load(resid[:], x_dram, x_loaded)
            for c in range(4):
                load(ctx_ring[:, c], ctx_dram[c], ctx_loaded[c])
                if c == 0:
                    for i in range(4):
                        lo = 0 if i < 3 else DH
                        load(wkv_sb[:, :, i, :], w_kv.rearrange("(c p) n -> p c n", p=P)[:, :, lo:lo + DH], wkv_loaded)
                    load(wq_sb, w_q.rearrange("(c p) n -> p c n", p=P), wq_loaded)
            with sp.Fori(1, NG // 4) as i:
                for c in range(4):
                    sp.wait_ge(s["ctx_tp"], i * 8 + (2 * c - 6))
                    load(ctx_ring[:, c], ctx_dram[bass.ds(4 * i + c, 1)].rearrange("g p t d -> p (g t) d"), ctx_loaded[c])
            qv = qparts.rearrange("p (c j) l -> p c j l", j=4)
            for b in range(B):
                sp.wait_ge(s["q_ready"], b + 1)
                cs = slice(b * DC, (b + 1) * DC)
                for j in range(4):
                    rows = slice(DH * j, DH * (j + 1))
                    load(qv[0:DH, cs, j, :], qhi[rows, cs, :], s[f"qparts_loaded{b}"])
                    load(qv[DH:2 * DH, cs, j, :], qhi[rows, cs, :], s[f"qparts_loaded{b}"])
                    load(qv[2 * DH:3 * DH, cs, j, :], qlo[rows, cs, :], s[f"qparts_loaded{b}"])
            for b in range(B):
                sp.wait_ge(s["box_ready"], b + 1)
                for c in range(b * DC, (b + 1) * DC):
                    load(qv[3 * DH:3 * DH + 1, c], box_hi[0:4, c], s["box_loaded"])
                    load(qv[3 * DH + 1:3 * DH + 2, c], box_lo[0:4, c], s["box_loaded"])
            sp.wait_ge(s["box_loaded"], 32 * B * DC)
            sp.wait_ge(s["flag_ready"], 1)
            with sp.If(sp.value_load(go_general[0:1, 0:1], min_val=0, max_val=1) > 0):
                sp.wait_ge(s["shift_ready"], 2)
                load(qparts[3 * DH:3 * DH + 1].rearrange("p u (t q) -> p (u t) q", q=P), shift_hi[:], s["shift_loaded"])
                load(qparts[3 * DH + 1:3 * DH + 2].rearrange("p u (t q) -> p (u t) q", q=P), shift_lo[:], s["shift_loaded"])
                sp.wait_ge(s["shift_loaded"], 32)
            sp.sem_inc(s["shift_final"], 1)
            sp.wait_ge(s["q_ready"], B)
            load(wc_sb, w_concat.rearrange("(c p) n -> p c n", p=P), s["wc_loaded"])
            load(bproj_sb[:], b_proj.rearrange("(a n) -> a n", a=1).broadcast_to([P, D]), s["bias_loaded"])
            sp.dma_start(bq_sb[:], b_qkv[0:D].rearrange("(c p) -> p c", p=P), allow_slow_non_contiguous=True)\
                .then_inc(s["bias_loaded"], 16)
            load(gate_sb[:], gate_w.rearrange("(c p) e -> p c e", p=P), s["bias_loaded"])
            sp.wait_ge(s["heads_ready"], TT)
            load(wqkv_sb, w_qkv.rearrange("(c p) n -> p c n", p=P), s["late_loaded"])
            load(wproj_sb, w_proj.rearrange("(c p) n -> p c n", p=P), s["late_loaded"])
            sp.wait_ge(s["concat_tp"], TT)
            load(bias_kv, b_qkv[D:3 * D].rearrange("(a n) -> a n", a=1).broadcast_to([P, 2 * D]), s["bias_loaded"])
            for e in range(E):
                load(wu_sb[:, e], w_u[e].rearrange("(c p) r -> p c r", p=P), s["ffnw_loaded"])
                load(wv_sb[:, e], w_v[e].rearrange("(c p) r -> p c r", p=P), s["ffnw_loaded"])
            load(wo_sb, w_o.rearrange("e r d -> r e d"), s["ffnw_loaded"])
            for t in range(TT):
                sp.wait_ge(s["ffn_added"], (E - 1) * TT + t + 1)
                load(out_dram[:, t], resid[:, t], s["out_done"])
            sp.wait_ge(s["out_done"], 16 * TT)

        @block.gpsimd
        def _(pool):
            done = [0]

            def step(ins):
                done[0] += 1
                ins.then_inc(consts_ready, 1)
                pool.wait_ge(consts_ready, done[0])

            step(nc.gpsimd.memset(ident[:], 0.0))
            step(nc.gpsimd.affine_select(out=ident[:], in_=ident[:], compare_op=ALU.not_equal, fill=1.0, base=0,
                                         pattern=[[-1, P]], channel_multiplier=1))
            step(nc.gpsimd.memset(kparts[3 * DH:3 * DH + 2, :], SHIFT_UNIT))
            step(nc.gpsimd.memset(ones[:], 1.0))
            step(nc.gpsimd.memset(zeros[:], 0.0))
            step(nc.gpsimd.memset(boxw[:], 0.0))
            step(nc.gpsimd.memset(blockmask[:], 0.0))
            for j in range(4):
                rows = slice(DH * j, DH * (j + 1))
                step(nc.gpsimd.memset(blockmask[rows, DH * j:DH * (j + 1)], 1.0))
                step(nc.gpsimd.memset(blockmask[rows, P + j:P + j + 1], 1.0))
            step(nc.gpsimd.memset(lower[:], 0.0))
            for e in range(1, E):
                step(nc.gpsimd.memset(lower[:, e, 0:e], 1.0))
            assert done[0] == CONSTS

        @block.scalar
        def _(act):
            def layernorm_std(k):
                act.wait_ge(s["bn_done"], k + 1)
                nc.scalar.activation(std[:], mv[:, :, 1], ACT.Sqrt).then_inc(s["std_done"], 1)

            layernorm_std(0)
            for i in range(2 * DC):
                b, c = divmod(i, DC)
                act.wait_ge(s["xT_tp"], i + 1)
                nc.scalar.copy(featT[:, c, b * L:(b + 1) * L], psum[:, i, :]).then_inc(s["xT_copied"], 1)
            for i in range(2 * DC):
                act.wait_ge(s["q_mm"], i + 1)
                nc.scalar.copy(qT[:, i], psum[:, i, :]).then_inc(s["q_copied"], 1)
            def copy_context(c, group):
                for half in range(2):
                    act.wait_ge(s["ctx_tp"], group * 2 + (half + 1))
                    if half == 0:
                        act.wait_ge(s["kv_mm"], group + 1)
                    nc.scalar.copy(ctxT[:, c % 2, 2 * half:2 * half + 2, :],
                                   psum[:, 2 * half:2 * half + 2, :]).then_inc(s["ctxT_copied"], 1)

            def copy_keys(c, group):
                act.wait_ge(s["kv_mm"], group + 3)
                nc.scalar.copy(kvT[:, bass.ds(group * N_BANK, N_BANK)], psum[:, 4 + c % 2, :])\
                    .then_inc(s["kv_copied"], 1)

            for c in range(4):
                copy_context(c, c)
                if c:
                    copy_keys(c - 1, c - 1)
            with act.Fori(1, NG // 4) as i:
                for c in range(4):
                    copy_context(c, i * 4 + c)
                    copy_keys((c - 1) % 4, i * 4 + (c - 1))
            copy_keys(3, NG - 1)
            for i in range(B * KT // 16):
                act.wait_ge(s["v_tp"], i + 1)
                nc.scalar.copy(v_sb[:, 16 * i:16 * (i + 1), 0:DH],
                               psum[:, i % 2, :].rearrange("p (k d) -> p k d", d=DH)).then_inc(s["v_hi"], 1)
            act.wait_ge(consts_ready, CONSTS)
            nc.scalar.activation(warm[:, 0:1], ident[:, 0:1], ACT.Exp).then_inc(s["act_link"], 1)
            def exp_round(step0):
                for j in range(NP):
                    act.wait_ge(s["scores_ready"], step0 + (j + 1))
                    act.wait_ge(s["prob_slot_free"], step0 + (j + 1))
                    sl = 2 * (j % 2)
                    nc.scalar.activation(prob[:, j], psum[:, sl:sl + 2, :].rearrange("p a n -> p (a n)"),
                                         ACT.Exp, scale=SCALE).then_inc(s["exp_done"], 1)

            def copy_sums(u, slot):
                act.wait_ge(s["prob_slot_free"], u * STEPS + (STEPS + NP))
                nc.scalar.copy(sums[:, bass.ds(u, 1)].rearrange("p u t c -> p (u t c)"),
                               psum[:, 4 + slot, 0:LT * OC]).then_inc(s["out_slot_free"], 1)

            def exp_unit(u, before=None):
                exp_round(u * STEPS)
                if before is not None:
                    copy_sums(*before)
                with act.Fori(1, STEPS // NP) as i:
                    exp_round(i * NP + u * STEPS)

            exp_unit(0)
            exp_unit(1, (0, 0))
            with act.Fori(1, UNITS // 2) as pair:
                exp_unit(pair * 2, (pair * 2 - 1, 1))
                exp_unit(pair * 2 + 1, (pair * 2, 0))
            copy_sums(UNITS - 1, 1)
            for i in range(TT):
                act.wait_ge(s["concat_tp"], i + 1)
                nc.scalar.activation(featT[:, :, i * P:(i + 1) * P],
                                     psum[:, i % 2, :].rearrange("p (c q) -> p c q", c=DC), ACT.Copy,
                                     scale=vpow[:, i // LT:i // LT + 1]).then_inc(s["concat_copied"], 1)
            layernorm_std(1)
            for i in range(2 * DC):
                b, c = divmod(i, DC)
                act.wait_ge(s["xT_tp"], 2 * DC + i + 1)
                nc.scalar.copy(featT[:, c, b * L:(b + 1) * L], psum[:, i, :]).then_inc(s["xT_copied"], 1)
            act.wait_ge(s["bias_loaded"], 64)
            for i in range(2 * DC):
                b, c = divmod(i, DC)
                act.wait_ge(s["qkv_q"], i + 1)
                if i >= 2:
                    act.wait_ge(s["qkv_qdone"], i - 1)
                nc.scalar.activation(ela[:, i % 2], psum[:, i % 2, :], ACT.Exp,
                                     bias=bq_sb[:, c:c + 1]).then_inc(s["qkv_qexp"], 1)
            for t in range(TT):
                act.wait_ge(s["qkv_kb"], t + 1)
                if t == 0:
                    act.wait_ge(s["qkv_qdone"], 2 * DC)
                else:
                    act.wait_ge(s["qkv_kdone"], max(t - 1, 1))
                nc.scalar.activation(ela[:, t % 2], kf[:, t], ACT.Exp).then_inc(s["qkv_kexp"], 1)
            for i in range(TT):
                act.wait_ge(s["la_tp"], i + 1)
                nc.scalar.copy(featT[:, :, i * P:(i + 1) * P],
                               psum[:, 4 + i % 2, :].rearrange("p (c q) -> p c q", c=DC)).then_inc(s["la_copied"], 1)
            layernorm_std(2)
            for i in range(2 * DC):
                b, c = divmod(i, DC)
                act.wait_ge(s["xT_tp"], 4 * DC + i + 1)
                nc.scalar.copy(featT[:, c, b * L:(b + 1) * L], psum[:, i, :]).then_inc(s["xT_copied"], 1)
            act.wait_ge(s["logit_done"], 1)
            nc.scalar.activation(ge[:], lg[:], ACT.Exp).then_inc(s["gate_exp"], 1)
            for i in range(E * B):
                act.wait_ge(s["ffn_u"], i + 1)
                if i >= 2:
                    act.wait_ge(s["ffn_s"], i - 1)
                nc.scalar.activation(ffe[:, i % 2], psum[:, i % 2, :], ACT.Exp, scale=-1.0).then_inc(s["ffn_exp"], 1)

        @block.vector
        def _(dve):
            n = [0]

            def link(ins):
                n[0] += 1
                ins.then_inc(s["dve_link"], 1)
                dve.wait_ge(s["dve_link"], n[0])

            def layernorm(k, dst):
                for t in range(TT):
                    last = nc.vector.bn_stats(bn6[:, t], resid[:, t])
                link(last)
                for t in range(TT):
                    last = nc.vector.bn_aggr(mv[:, t], bn6[:, t])
                link(last)
                nc.vector.tensor_scalar(mv[:, :, 1], mv[:, :, 1], EPS_LN, None, ALU.add).then_inc(s["bn_done"], 1)
                dve.wait_ge(s["std_done"], k + 1)
                link(nc.vector.reciprocal(rstd[:], std[:]))
                for t in range(TT):
                    nc.vector.tensor_scalar(dst[:, t], resid[:, t], mv[:, t, 0:1], rstd[:, t:t + 1],
                                            ALU.subtract, ALU.mult).then_inc(s["xn_ready"], 1)

            dve.wait_ge(x_loaded, 16)
            layernorm(0, xnorm)
            for b in range(B):
                with dve.Fori(0, GB // 4) as i:
                    for c in range(4):
                        dve.wait_ge(s["kv_copied"], (b * GB + c + 1) + i * 4)
                        src = kvT[:, bass.ds((b * GB + c) * N_BANK + i * (4 * N_BANK), N_BANK)]
                        nc.vector.tensor_reduce(kstat[:, 2, bass.ds(b * GB + c + i * 4, 1)], src, AX, ALU.add)
                        nc.vector.tensor_reduce(kstat[:, 0, bass.ds(b * GB + c + i * 4, 1)], src, AX, ALU.max)
                        nc.vector.tensor_reduce(kstat[:, 1, bass.ds(b * GB + c + i * 4, 1)], src, AX, ALU.min)\
                            .then_inc(s["stat_done"], 1)
                dve.wait_ge(s["stat_done"], GB * (b + 1))
                gs = slice(b * GB, (b + 1) * GB)
                nc.vector.tensor_reduce(kext[:, b, 0:1], kstat[:, 0, gs], AX, ALU.max)
                nc.vector.tensor_reduce(kext[:, b, 2:3], kstat[:, 2, gs], AX, ALU.add)
                link(nc.vector.tensor_reduce(kext[:, b, 1:2], kstat[:, 1, gs], AX, ALU.min))
                bb = slice(b, b + 1)
                link(nc.vector.scalar_tensor_tensor(kabs[:, bb], kext[:, b, 1:2], -1.0, kext[:, b, 0:1],
                                                    ALU.mult, ALU.max))
                link(nc.vector.tensor_scalar(kabs[:, bb], kabs[:, bb], 1e-30, None, ALU.max))
                link(nc.vector.tensor_scalar(kpow[:, bb].bitcast(I32), kabs[:, bb].bitcast(I32), EXPONENT_BITS, None,
                                             ALU.bitwise_and))
                link(nc.vector.reciprocal(kinv[:, bb], kpow[:, bb]))
                for j in range(4):
                    rows = slice(DH * j, DH * (j + 1))
                    nc.vector.tensor_copy(qpow[rows, bb], kpow[0:DH, bb])
                    last = nc.vector.tensor_copy(vpow[rows, bb], kpow[3 * DH:4 * DH, bb])
                link(last)
                link(nc.vector.tensor_scalar(kext[:, b, 2:3], kext[:, b, 2:3], 1.0 / M, None, ALU.mult))
                link(nc.vector.tensor_scalar(kext[:, b], kext[:, b], kinv[:, bb], None, ALU.mult))
                nc.vector.tensor_scalar(kbox[:, b, 0:1], kext[:, b, 0:1], -1.0 / SHIFT_UNIT, None, ALU.mult)
                nc.vector.tensor_tensor(kbox[:, b, 1:2], kext[:, b, 0:1], kext[:, b, 2:3], ALU.subtract)
                nc.vector.tensor_scalar(kbox[:, b, 2:3], kext[:, b, 1:2], 1.0 / SHIFT_UNIT, None, ALU.mult)
                link(nc.vector.tensor_tensor(kbox[:, b, 3:4], kext[:, b, 2:3], kext[:, b, 1:2], ALU.subtract))
                for j in range(4):
                    last = nc.vector.tensor_copy(kbox4[DH * j:DH * (j + 1), b], kbox[0:DH, b])
                link(last)
                dve.wait_ge(consts_ready, CONSTS)
                for k in range(4):
                    last = nc.vector.tensor_scalar(boxw[:, b, k // 2, DH * (k % 2):DH * (k % 2) + 4], blockmask[:, P:P + 4],
                                                   kbox4[:, b, k:k + 1], None, ALU.mult)
                link(last)
                keys = slice(b * M, (b + 1) * M)
                link(nc.vector.tensor_scalar(kparts[0:3 * DH, keys], kvT[0:3 * DH, keys], kinv[0:3 * DH, bb], None, ALU.mult))
                nc.vector.scalar_tensor_tensor(kparts[DH:2 * DH, keys], kvT[DH:2 * DH, keys], kinv[DH:2 * DH, bb],
                                               kparts[DH:2 * DH, keys], ALU.mult, ALU.subtract)\
                    .then_inc(s["kparts_ready"], 1)
                nc.vector.tensor_scalar(kvT[3 * DH:4 * DH, keys], kvT[3 * DH:4 * DH, keys], kinv[3 * DH:4 * DH, bb],
                                        None, ALU.mult).then_inc(s["v_scaled"], 1)
            for i in range(B * KT // 16):
                dve.wait_ge(s["v_hi"], i + 1)
                if i == 0:
                    nc.vector.memset(v_sb[:, :, 2 * DH:OC], 1.0)
                tiles = slice(16 * i, 16 * (i + 1))
                nc.vector.tensor_tensor(v_sb[:, tiles, DH:2 * DH], psum[:, i % 2, :].rearrange("p (k d) -> p k d", d=DH),
                                        v_sb[:, tiles, 0:DH], ALU.subtract).then_inc(s["v_copied"], 1)
            for b in range(B):
                cs = slice(b * DC, (b + 1) * DC)
                dve.wait_ge(s["q_copied"], DC * (b + 1))
                link(nc.vector.tensor_scalar(qhi[:, cs], qT[:, cs], qpow[:, b:b + 1], None, ALU.mult))
                nc.vector.scalar_tensor_tensor(qlo[:, cs], qT[:, cs], qpow[:, b:b + 1], qhi[:, cs],
                                               ALU.mult, ALU.subtract).then_inc(s["q_ready"], 1)
            for b in range(B):
                cs = slice(b * DC, (b + 1) * DC)
                if b:
                    dve.wait_ge(s["box_mm"], b * DC)
                nc.vector.tensor_scalar(qpos, qT[:, cs], qpow[:, b:b + 1], 0.0, ALU.mult, ALU.max)
                link(nc.vector.tensor_scalar(qneg, qT[:, cs], qpow[:, b:b + 1], 0.0, ALU.mult, ALU.min))
                nc.vector.tensor_scalar(qneg, qneg, -1.0, None, ALU.mult).then_inc(s["qneg_ready"], 1)
                dve.wait_ge(s["box_mm"], (b + 1) * DC)
                nc.vector.tensor_copy(box_hi[0:4, cs], psum[0:4, cs, :]).then_inc(s["box_hi_ready"], 1)
                dve.wait_ge(s["box_hi_ready"], b + 1)
                nc.vector.tensor_tensor(box_lo[0:4, cs], psum[0:4, cs, :], box_hi[0:4, cs], ALU.subtract)\
                    .then_inc(s["box_ready"], 1)
                link(nc.vector.tensor_reduce(gap[DH:DH + 4, b:b + 1], psum[DH:DH + 4, cs, :].rearrange("p a n -> p (a n)"),
                                             AX, ALU.max))
            link(nc.vector.tensor_reduce(gap_ok[DH:DH + 4, 0:1], gap[DH:DH + 4, :], AX, ALU.max))
            nc.vector.tensor_scalar(gap_ok[DH:DH + 4, 1:2], gap_ok[DH:DH + 4, 0:1], GAP_LIMIT / SCALE, None, ALU.is_le)\
                .then_inc(s["gap_ready"], 1)
            dve.wait_ge(s["gap_count"], 1)
            nc.vector.tensor_scalar(go_general[0:1, 0:1], psum[0:1, 0, 0:1], 3.5, None, ALU.is_lt)\
                .then_inc(s["flag_ready"], 1)
            dve.wait_ge(s["flag_ready"], 1)
            with dve.If(dve.value_load(go_general[0:1, 0:1], min_val=0, max_val=1) > 0):
                for b in range(B):
                    with dve.Fori(0, H) as h:
                        for t in range(LT):
                            for k in range(4):
                                i0 = b * H * 16 + t * 4 + k
                                dve.wait_ge(s["max_scores"], h * 16 + i0 + 1)
                                sl = 4 * (k % 2)
                                nc.vector.tensor_reduce(rowmax[:, bass.ds(h + b * H, 1), t, k:k + 1],
                                                        psum[:, sl:sl + 4, :].rearrange("p a n -> p (a n)"),
                                                        AX, ALU.max).then_inc(s["max_read"], 1)
                dve.wait_ge(s["max_read"], 2 + UNITS * 16)
                nc.vector.tensor_reduce(shiftc[:], rowmax[:].rearrange("p u t k -> p (u t) k"), AX, ALU.max)\
                    .then_inc(s["shift_cols"], 1)
                dve.wait_ge(s["shift_tp"], 1)
                nc.vector.tensor_scalar(shift_hi[:], psum[:, 0, 0:P], -1.0 / SHIFT_UNIT, None, ALU.mult)\
                    .then_inc(s["shift_ready"], 1)
                dve.wait_ge(s["shift_ready"], 1)
                nc.vector.scalar_tensor_tensor(shift_lo[:], psum[:, 0, 0:P], -1.0 / SHIFT_UNIT, shift_hi[:],
                                               ALU.mult, ALU.subtract).then_inc(s["shift_ready"], 1)


            with dve.Fori(0, UNITS * STEPS // NP) as i:
                for j in range(0, NP, 2):
                    dve.wait_ge(s["exp_done"], i * NP + (j + 4))
                    both = prob[:, j:j + 2].rearrange("p a n -> p (a n)")
                    hi = both.bitcast(BF16).rearrange("p (n two) -> p n two", two=2)[:, :, 1]
                    nc.vector.tensor_tensor(prob_lo[:, j:j + 2].rearrange("p a n -> p (a n)"), both, hi, ALU.subtract)\
                        .then_inc(s["lo_ready"], 1)
            dve.wait_ge(s["out_slot_free"], UNITS + 2)
            nc.vector.reciprocal(sum_rec, sums[:, :, :, 2 * DH]).then_inc(s["sums_done"], 1)
            nc.vector.tensor_tensor(sums[:, :, :, 0:DH], sums[:, :, :, 0:DH], sums[:, :, :, DH:2 * DH], ALU.add)\
                .then_inc(s["sums_done"], 1)
            dve.wait_ge(s["sums_done"], 2)
            for b in range(B):
                for t in range(LT):
                    us = slice(b * H, (b + 1) * H)
                    nc.vector.tensor_tensor(heads[:, b * LT + t].rearrange("p (h d) -> p h d", d=DH), sums[:, us, t, 0:DH],
                                            sum_rec[:, us, t:t + 1].broadcast_to([P, H, DH]), ALU.mult)\
                        .then_inc(s["heads_ready"], 1)

            for t in range(TT):
                dve.wait_ge(s["concat_mm"], t + 1)
                nc.vector.tensor_tensor(resid[:, t], psum[:, 2 + t % 2, :], resid[:, t], ALU.add)\
                    .then_inc(s["concat_added"], 1)
            dve.wait_ge(s["concat_added"], TT)
            layernorm(1, xn2)
            dve.wait_ge(s["bias_loaded"], 64)
            for i in range(2 * DC):
                b, c = divmod(i, DC)
                dve.wait_ge(s["qkv_qexp"], i + 1)
                link(nc.vector.tensor_scalar(elb[:, 0], psum[:, i % 2, :], bq_sb[:, c:c + 1], 0.0, ALU.add, ALU.max))
                nc.vector.scalar_tensor_tensor(qf[:, c, b * L:(b + 1) * L], ela[:, i % 2], 1.0, elb[:, 0],
                                               ALU.min, ALU.add).then_inc(s["qkv_qdone"], 1)
                dve.wait_ge(s["qkv_qdone"], i + 1)
            link(nc.vector.memset(vf[:, :, :, P:P + 1], 1.0))
            for t in range(TT):
                dve.wait_ge(s["qkv_k"], t + 1)
                nc.vector.tensor_tensor(kf[:, t], psum[:, 2 + t % 2, :], bias_kv[:, 0:D], ALU.add).then_inc(s["qkv_kb"], 1)
                dve.wait_ge(s["qkv_v"], t + 1)
                nc.vector.tensor_tensor(vf[:, t, :, 0:P], psum[:, 4 + t % 2, :].rearrange("p (c n) -> p c n", c=DC),
                                        bias_kv[:, D:2 * D].rearrange("p (c n) -> p c n", c=DC), ALU.add)\
                    .then_inc(s["qkv_vdone"], 1)
                dve.wait_ge(s["qkv_kexp"], t + 1)
                link(nc.vector.tensor_scalar(kf[:, t], kf[:, t], 0.0, None, ALU.max))
                nc.vector.scalar_tensor_tensor(kf[:, t], ela[:, t % 2], 1.0, kf[:, t], ALU.min, ALU.add)\
                    .then_inc(s["qkv_kdone"], 1)
            for i in range(2 * DC):
                dve.wait_ge(s["state_mm"], i + 1)
                ps = psum[:, i % 2, :]
                nc.vector.tensor_tensor(state[:, i, 0:P], ps[:, 0:P], blockmask[:, 0:P], ALU.mult)
                nc.vector.tensor_scalar(state[:, i, P:P + 4], blockmask[:, P:P + 4], ps[:, P:P + 1], None, ALU.mult)\
                    .then_inc(s["state_done"], 1)
            for t in range(TT):
                dve.wait_ge(s["la_mm"], t + 1)
                sl = 2 * (t % 2)
                o = psum[:, sl:sl + 2, 0:2 * (P + 4)].rearrange("p a (c n) -> p a c n", c=2)
                link(nc.vector.tensor_scalar(zden[:], o[:, :, :, P:P + 4], EPS_Z, None, ALU.add))
                link(nc.vector.reciprocal(zden[:], zden[:]))
                for a in range(2):
                    last = nc.vector.tensor_tensor(
                        la[:, t, a * 256:(a + 1) * 256].rearrange("p (c j d) -> p c j d", c=2, j=4),
                        o[:, a, :, 0:P].rearrange("p c (j d) -> p c j d", j=4),
                        zden[:, a].rearrange("p c (j o) -> p c j o", o=1).broadcast_to([P, 2, 4, DH]), ALU.mult)
                last.then_inc(s["la_done"], 1)
                dve.wait_ge(s["la_done"], t + 1)
            for t in range(TT):
                nc.vector.tensor_tensor(resid[:, t], resid[:, t], bproj_sb[:], ALU.add).then_inc(s["dve_link"], 1)
                n[0] += 1
            dve.wait_ge(s["dve_link"], n[0])
            for t in range(TT):
                dve.wait_ge(s["proj_mm"], t + 1)
                nc.vector.tensor_tensor(resid[:, t], psum[:, 6 + t % 2, :], resid[:, t], ALU.add)\
                    .then_inc(s["proj_added"], 1)
            dve.wait_ge(s["proj_added"], TT)
            layernorm(2, xn2)
            dve.wait_ge(consts_ready, CONSTS)
            dve.wait_ge(s["logit_mm"], 1)
            link(nc.vector.tensor_copy(lg[:], psum[:, 7, 0:TT * E].rearrange("p (t e) -> p t e", e=E)))
            flat = lg[:].rearrange("p t e -> p (t e)")
            for e in range(E):
                le = lg[:, :, e:e + 1].broadcast_to([P, TT, E])
                ca = cmpa.rearrange("p (t e) j -> p t e j", e=E)[:, :, e, :]
                cb = cmpb.rearrange("p (t e) j -> p t e j", e=E)[:, :, e, :]
                nc.vector.tensor_tensor(ca, lg[:], le, ALU.is_gt)
                link(nc.vector.tensor_tensor(cb, lg[:], le, ALU.is_equal))
                link(nc.vector.tensor_tensor(cb, cb, lower[:, e:e + 1, :].broadcast_to([P, TT, E]), ALU.mult))
            link(nc.vector.tensor_tensor(cmpa, cmpa, cmpb, ALU.add))
            link(nc.vector.tensor_reduce(rank[:].rearrange("p t e -> p (t e)"), cmpa, AX, ALU.add))
            link(nc.vector.tensor_scalar(rank[:], rank[:], 1.5, None, ALU.is_lt))
            link(nc.vector.tensor_reduce(gmax[:], lg[:], AX, ALU.max))
            nc.vector.tensor_tensor(lg[:], lg[:], gmax[:].rearrange("p (t o) -> p t o", o=1).broadcast_to([P, TT, E]),
                                    ALU.subtract).then_inc(s["logit_done"], 1)
            dve.wait_ge(s["gate_exp"], 1)
            link(nc.vector.tensor_tensor(gate[:], ge[:], rank[:], ALU.mult))
            link(nc.vector.tensor_reduce(gsum[:], gate[:], AX, ALU.add))
            link(nc.vector.reciprocal(gsum[:], gsum[:]))
            link(nc.vector.tensor_tensor(gate[:], gate[:],
                                         gsum[:].rearrange("p (t o) -> p t o", o=1).broadcast_to([P, TT, E]), ALU.mult))

            def add_experts(i):
                e, b = divmod(i, B)
                for t in range(LT):
                    k = i * LT + t
                    dve.wait_ge(s["ffn_y"], k + 1)
                    tok = b * LT + t
                    if e:
                        dve.wait_ge(s["ffn_added"], k - B * LT + 1)
                    nc.vector.scalar_tensor_tensor(resid[:, tok], psum[:, 4 + k % 4, :], gate[:, tok, e:e + 1],
                                                   resid[:, tok], ALU.mult, ALU.add).then_inc(s["ffn_added"], 1)

            for i in range(E * B):
                dve.wait_ge(s["ffn_exp"], i + 1)
                link(nc.vector.tensor_scalar(ffe[:, i % 2], ffe[:, i % 2], 1.0, None, ALU.add))
                link(nc.vector.reciprocal(ffr[:, i % 2], ffe[:, i % 2]))
                link(nc.vector.tensor_tensor(fft[:, i % 2], psum[:, i % 2, :], ffr[:, i % 2], ALU.mult))
                dve.wait_ge(s["ffn_v"], i + 1)
                nc.vector.tensor_tensor(ffs[:, i % 2], psum[:, 2 + i % 2, :], fft[:, i % 2], ALU.mult)\
                    .then_inc(s["ffn_s"], 1)
                if i >= 1:
                    add_experts(i - 1)
            add_experts(E * B - 1)

        @block.tensor
        def _(pe):
            def transpose_tokens(k, src):
                for i in range(2 * DC):
                    b, c = divmod(i, DC)
                    if c == 0:
                        pe.wait_ge(s["xn_ready"], k * TT + (b + 1) * LT)
                    for t in range(LT):
                        last = nc.tensor.transpose(psum[:, i, t * P:(t + 1) * P],
                                                   src[:, b * LT + t, c * P:(c + 1) * P], ident[:])
                    last.then_inc(s["xT_tp"], 1)

            pe.wait_ge(consts_ready, 2)
            transpose_tokens(0, xnorm)
            pe.wait_ge(wq_loaded, 16)
            pe.wait_ge(s["xT_copied"], 2 * DC)
            for i in range(2 * DC):
                b, m = divmod(i, DC)
                for c in range(DC):
                    last = nc.tensor.matmul(psum[:, i, :], wq_sb[:, c, m * P:(m + 1) * P],
                                            featT[:, c, b * L:(b + 1) * L], start=(c == 0), stop=(c == DC - 1))
                last.then_inc(s["q_mm"], 1)
            pe.wait_ge(s["q_copied"], 2 * DC)
            pe.wait_ge(wkv_loaded, 64)
            pe.sem_inc(s["kv_mm"], 2)

            def transpose_context(c, loaded, copied):
                pe.wait_ge(ctx_loaded[c], loaded)
                for half in range(2):
                    if copied is not None:
                        pe.wait_ge(s["ctxT_copied"], copied + half)
                    for cc in range(2):
                        for t in range(4):
                            f = 2 * half + cc
                            last = nc.tensor.transpose(psum[:, f, t * P:(t + 1) * P],
                                                       ctx_ring[:, c, t, f * P:(f + 1) * P], ident[:])
                    last.then_inc(s["ctx_tp"], 1)

            def multiply_context(c, copied, free):
                pe.wait_ge(s["ctxT_copied"], copied)
                if free is not None:
                    pe.wait_ge(s["kv_copied"], free)
                for f in range(DC):
                    last = nc.tensor.matmul(psum[:, 4 + c % 2, :], wkv_sb[:, f].rearrange("p a n -> p (a n)"),
                                            ctxT[:, c % 2, f, :], start=(f == 0), stop=(f == DC - 1))
                last.then_inc(s["kv_mm"], 1)

            transpose_context(0, 16, None)
            for c in range(4):
                if c < 3:
                    transpose_context(c + 1, 16, 2 * c + 1)
                else:
                    transpose_context(0, 32, 2 * c + 1)
                multiply_context(c, 2 * c + 2, c - 1 if c >= 2 else None)
            with pe.Fori(1, NG // 4 - 1) as i:
                for c in range(4):
                    if c < 3:
                        transpose_context(c + 1, i * 16 + 16, i * 8 + 2 * c + 1)
                    else:
                        transpose_context(0, i * 16 + 32, i * 8 + 2 * c + 1)
                    multiply_context(c, i * 8 + 2 * c + 2, i * 4 + c - 1)
            last_round = NG // 4 - 1
            for c in range(4):
                if c < 3:
                    transpose_context(c + 1, last_round * 16 + 16, last_round * 8 + 2 * c + 1)
                multiply_context(c, last_round * 8 + 2 * c + 2, last_round * 4 + c - 1)

            for i in range(B * KT // 16):
                if i % (KT // 16) == 0:
                    pe.wait_ge(s["v_scaled"], i // (KT // 16) + 1)
                if i >= 2:
                    pe.wait_ge(s["v_copied"], i - 1)
                else:
                    pe.wait_ge(s["ctxT_copied"], 2 * NG)
                for k in range(16):
                    last = nc.tensor.transpose(psum[:, i % 2, k * DH:(k + 1) * DH],
                                               kvT[3 * DH:4 * DH, (16 * i + k) * P:(16 * i + k + 1) * P],
                                               ident[3 * DH:4 * DH, 3 * DH:4 * DH])
                last.then_inc(s["v_tp"], 1)

            pe.wait_ge(s["kparts_ready"], B)
            pe.wait_ge(s["v_copied"], B * KT // 16)
            pe.wait_ge(s["kv_copied"], NG)
            for i in range(2 * DC):
                b, c = divmod(i, DC)
                pe.wait_ge(s["qneg_ready"], b + 1)
                nc.tensor.matmul(psum[0:DH + 4, i, :], boxw[:, b, 0], qpos[:, c], start=True, stop=False)
                nc.tensor.matmul(psum[0:DH + 4, i, :], boxw[:, b, 1], qneg[:, c], start=False, stop=True)\
                    .then_inc(s["box_mm"], 1)
            pe.wait_ge(s["gap_ready"], 1)
            nc.tensor.matmul(psum[0:1, 0, 0:1], gap_ok[DH:DH + 4, 1:2], ones[DH:DH + 4, 0:1], start=True, stop=True)\
                .then_inc(s["gap_count"], 1)
            pe.wait_ge(s["flag_ready"], 1)
            for b in range(B):
                pe.wait_ge(s[f"qparts_loaded{b}"], 16 * 12)
            with pe.If(pe.value_load(go_general[0:1, 0:1], min_val=0, max_val=1) > 0):
                pe.sem_inc(s["max_read"], 2)
                for b in range(B):
                    with pe.Fori(0, H) as h:
                        for t in range(LT):
                            for k in range(4):
                                pe.wait_ge(s["max_read"], h * 16 + (b * H * 16 + t * 4 + k + 1))
                                for a in range(4):
                                    lhs = qparts[0:3 * DH, bass.ds(h + b * H, 1), t * P:(t + 1) * P]
                                    last = nc.tensor.matmul(psum[:, 4 * (k % 2) + a, :], lhs.rearrange("p u q -> p (u q)"),
                                                            kparts[0:3 * DH, b * M + (4 * k + a) * N_BANK:
                                                                   b * M + (4 * k + a + 1) * N_BANK], start=True, stop=True)
                                last.then_inc(s["max_scores"], 1)
                pe.wait_ge(s["shift_cols"], 1)
                nc.tensor.transpose(psum[:, 0, 0:P], shiftc[:], ident[:]).then_inc(s["shift_tp"], 1)

            pe.wait_ge(s["shift_final"], 1)

            pe.sem_inc(s["exp_done"], 2)
            pe.sem_inc(s["prob_slot_free"], NP)
            pe.sem_inc(s["out_slot_free"], 2)

            def scores(b, h, step, j, count):
                pe.wait_ge(s["exp_done"], count)
                q = qparts[0:3 * DH + 2, bass.ds(h + b * H, 1), :].rearrange("p u q -> p (u q)")
                for a in range(2):
                    keys = kparts[0:3 * DH + 2, bass.ds(step * (2 * P) + (b * M + a * P), P)]
                    last = nc.tensor.matmul(psum[:, 2 * (j % 2) + a, :], keys, q, start=True, stop=True)
                last.then_inc(s["scores_ready"], 1)

            def values(b, step, j, pairs_done, slot, last_step):
                if j % 2 == 0:
                    pe.wait_ge(s["lo_ready"], pairs_done)
                hi = prob[:, j].bitcast(BF16).rearrange("p (n two) -> p n two", two=2)[:, :, 1]
                for a in range(2):
                    v = v_sb[:, bass.ds(step * 2 + (b * KT + a), 1), :].rearrange("p k c -> p (k c)")
                    for t in range(LT):
                        q = slice(a * N_BANK + t * P, a * N_BANK + (t + 1) * P)
                        for part, lhs in enumerate((hi[:, q], prob_lo[:, j, q])):
                            mm = nc.tensor.matmul(psum[:, 4 + slot, t * OC:(t + 1) * OC], lhs, v, start=False,
                                                  stop=(last_step and a == 1 and part == 1), skip_group_check=True)
                mm.then_inc(s["prob_slot_free"], 1)

            def unit(b, h, slot, nxt):
                u = h + b * H
                pe.wait_ge(s["out_slot_free"], u + 1)
                nc.tensor.matmul(psum[:, 4 + slot, 0:LT * OC], zeros[:], kparts[0:DH, 0:LT * OC], start=True, stop=False,
                                 skip_group_check=True)

                def round_of_steps(i, last_round):
                    for j in range(NP):
                        step = i * NP + j
                        count = u * STEPS + step
                        if not (last_round and j >= NP - LEAD):
                            scores(b, h, step + LEAD, j + LEAD, count + (LEAD + 1))
                        elif nxt is not None:
                            scores(nxt[0], nxt[1], j - (NP - LEAD), j + LEAD, count + (LEAD + 1))
                        values(b, step, j, u * (STEPS // 2) + i * (NP // 2) + (j // 2 + 1), slot, last_round and j == NP - 1)

                with pe.Fori(0, STEPS // NP - 1) as i:
                    round_of_steps(i, False)
                round_of_steps(STEPS // NP - 1, True)

            pe.wait_ge(consts_ready, CONSTS)
            for j in range(LEAD):
                scores(0, 0, j, j, j + 1)
            for b in range(B):
                with pe.Fori(0, H // 2 - 1) as pair:
                    unit(b, pair * 2, 0, (b, pair * 2 + 1))
                    unit(b, pair * 2 + 1, 1, (b, pair * 2 + 2))
                unit(b, H - 2, 0, (b, H - 1))
                unit(b, H - 1, 1, (b + 1, 0) if b + 1 < B else None)

            pe.wait_ge(s["wc_loaded"], 16)

            def token_products(src_rows, dst, weights, cols, signal):
                for c in range(DC):
                    last = nc.tensor.matmul(dst, featT[:, c, src_rows], weights[:, c, cols],
                                            start=(c == 0), stop=(c == DC - 1))
                last.then_inc(signal, 1)

            def concat(t):
                pe.wait_ge(s["concat_copied"], t + 1)
                if t >= 2:
                    pe.wait_ge(s["concat_added"], t - 1)
                token_products(slice(t * P, (t + 1) * P), psum[:, 2 + t % 2, :], wc_sb, slice(0, D), s["concat_mm"])

            for t in range(TT):
                pe.wait_ge(s["heads_ready"], t + 1)
                if t >= 2:
                    pe.wait_ge(s["concat_copied"], t - 1)
                for c in range(DC):
                    last = nc.tensor.transpose(psum[:, t % 2, c * P:(c + 1) * P], heads[:, t, c * P:(c + 1) * P], ident[:])
                last.then_inc(s["concat_tp"], 1)
                if t:
                    concat(t - 1)
            concat(TT - 1)

            transpose_tokens(1, xn2)
            pe.wait_ge(s["late_loaded"], 32)
            pe.wait_ge(s["xT_copied"], 4 * DC)
            for i in range(2 * DC):
                b, m = divmod(i, DC)
                if i >= 2:
                    pe.wait_ge(s["qkv_qdone"], i - 1)
                for c in range(DC):
                    last = nc.tensor.matmul(psum[:, i % 2, :], wqkv_sb[:, c, m * P:(m + 1) * P],
                                            featT[:, c, b * L:(b + 1) * L], start=(c == 0), stop=(c == DC - 1))
                last.then_inc(s["qkv_q"], 1)
            for t in range(TT):
                rows = slice(t * P, (t + 1) * P)
                if t >= 2:
                    pe.wait_ge(s["qkv_kb"], t - 1)
                token_products(rows, psum[:, 2 + t % 2, :], wqkv_sb, slice(D, 2 * D), s["qkv_k"])
                if t >= 2:
                    pe.wait_ge(s["qkv_vdone"], t - 1)
                token_products(rows, psum[:, 4 + t % 2, :], wqkv_sb, slice(2 * D, 3 * D), s["qkv_v"])
            pe.wait_ge(s["qkv_qdone"], 2 * DC)
            for i in range(2 * DC):
                b, c = divmod(i, DC)
                pe.wait_ge(s["qkv_kdone"], (b + 1) * LT)
                pe.wait_ge(s["qkv_vdone"], (b + 1) * LT)
                if i >= 2:
                    pe.wait_ge(s["state_done"], i - 1)
                for t in range(LT):
                    last = nc.tensor.matmul(psum[:, i % 2, 0:P + 1], kf[:, b * LT + t, c * P:(c + 1) * P],
                                            vf[:, b * LT + t, c, :], start=(t == 0), stop=(t == LT - 1))
                last.then_inc(s["state_mm"], 1)
            pe.wait_ge(s["state_done"], 2 * DC)
            for t in range(TT):
                if t >= 2:
                    pe.wait_ge(s["la_done"], t - 1)
                for c in range(DC):
                    last = nc.tensor.matmul(psum[:, 2 * (t % 2) + c // 2, (c % 2) * (P + 4):(c % 2 + 1) * (P + 4)],
                                            qf[:, c, t * P:(t + 1) * P], state[:, (t // LT) * DC + c, :],
                                            start=True, stop=True)
                last.then_inc(s["la_mm"], 1)

            def project(t):
                pe.wait_ge(s["la_copied"], t + 1)
                if t >= 2:
                    pe.wait_ge(s["proj_added"], t - 1)
                token_products(slice(t * P, (t + 1) * P), psum[:, 6 + t % 2, :], wproj_sb, slice(0, D), s["proj_mm"])

            for t in range(TT):
                pe.wait_ge(s["la_done"], t + 1)
                if t >= 2:
                    pe.wait_ge(s["la_copied"], t - 1)
                for c in range(DC):
                    last = nc.tensor.transpose(psum[:, 4 + t % 2, c * P:(c + 1) * P], la[:, t, c * P:(c + 1) * P], ident[:])
                last.then_inc(s["la_tp"], 1)
                if t:
                    project(t - 1)
            project(TT - 1)

            transpose_tokens(2, xn2)
            pe.wait_ge(s["xT_copied"], 6 * DC)
            for t in range(TT):
                for c in range(DC):
                    last = nc.tensor.matmul(psum[:, 7, t * E:(t + 1) * E], featT[:, c, t * P:(t + 1) * P],
                                            gate_sb[:, c, :], start=(c == 0), stop=(c == DC - 1))
            last.then_inc(s["logit_mm"], 1)
            pe.wait_ge(s["ffnw_loaded"], 16 * (2 * E + 1))
            pe.wait_ge(s["logit_done"], 1)

            def expert_out(i):
                e, b = divmod(i, B)
                pe.wait_ge(s["ffn_s"], i + 1)
                for t in range(LT):
                    k = i * LT + t
                    if k >= 4:
                        pe.wait_ge(s["ffn_added"], k - 3)
                    nc.tensor.matmul(psum[:, 4 + k % 4, :], ffs[:, i % 2, t * P:(t + 1) * P], wo_sb[:, e, :],
                                     start=True, stop=True).then_inc(s["ffn_y"], 1)

            for i in range(E * B):
                e, b = divmod(i, B)
                if i >= 2:
                    pe.wait_ge(s["ffn_s"], i - 1)
                for bank, weights, signal in ((0, wu_sb, s["ffn_u"]), (2, wv_sb, s["ffn_v"])):
                    for c in range(DC):
                        last = nc.tensor.matmul(psum[:, bank + i % 2, :], weights[:, e, c, :],
                                                featT[:, c, b * L:(b + 1) * L], start=(c == 0), stop=(c == DC - 1))
                    last.then_inc(signal, 1)
                if i:
                    expert_out(i - 1)
            expert_out(E * B - 1)


_INS = ['x', 'ctx_1024', 'L0_xattn_w_q', 'L0_xattn_w_kv', 'L0_xattn_w_concat', 'L0_attn_w_qkv', 'L0_attn_b_qkv',
        'L0_attn_w_proj', 'L0_attn_b_proj', 'L0_ffn_gate_w', 'L0_ffn_Wu', 'L0_ffn_Wv', 'L0_ffn_Wo']
_OUTS = [((2, 512, 512), 'float32')]


def kernel(**inputs):
    import numpy as _np
    import concourse.bacc as _bacc
    from concourse import mybir as _mybir
    from concourse.bass_utils import run_bass_kernel_spmd as _run

    nc = _bacc.Bacc("TRN2", target_bir_lowering=False, num_devices=1)
    arrays, args = {}, []
    for name in _INS:
        a = _np.ascontiguousarray(inputs[name])
        arrays[f"in_{name}_dram"] = a
        args.append(nc.dram_tensor(f"in_{name}_dram", a.shape, _mybir.dt.from_np(a.dtype), kind="ExternalInput").ap())
    for i, (shape, dtype) in enumerate(_OUTS):
        dt = _mybir.dt.from_np(_np.dtype(dtype))
        args.append(nc.dram_tensor(f"out_{i}_dram", shape, dt, kind="ExternalOutput").ap())
    perceiver_block(nc, *args)
    r = _run(nc, [arrays], core_ids=[0])
    got = tuple(r.results[0][f"out_{i}_dram"] for i in range(len(_OUTS)))
    return got[0]
```

```python
from contextlib import ExitStack

import concourse.bass as bass
from concourse import mybir

ALU = mybir.AluOpType
ACT = mybir.ActivationFunctionType
F32 = mybir.dt.float32
F32R = mybir.dt.float32r
F16 = mybir.dt.float16
BF16 = mybir.dt.bfloat16
I32 = mybir.dt.int32
AX = mybir.AxisListType.X

P = 128
N_BANK = 512
DH = 32
SHIFT_UNIT = 64.0
EPS_LN = 1e-5
EPS_Z = 1e-8
EXPONENT_BITS = 0x7F800000
GAP_LIMIT = 60.0


def perceiver_block(nc, x, ctx_in, w_q, w_kv, w_concat, w_qkv, b_qkv, w_proj, b_proj, gate_w, w_u, w_v, w_o, out):
    B, L, D = x.shape
    M = ctx_in.shape[1]
    H = D // DH
    E, _, R = w_u.shape
    DC = D // P
    LT = L // P
    TT = B * LT
    NG = B * M // N_BANK
    GB = NG // B
    KT = M // P
    UNITS = B * H
    STEPS = KT // 2
    NP = 8
    LEAD = 5
    SCALE = float(DH) ** -0.5
    CONSTS = 2 + 4 + 9 + E
    OC = 2 * DH + 1

    with ExitStack() as stack:
        def sb(name, shape, dt=F32):
            return stack.enter_context(nc.sbuf_tensor(name, shape, dt))

        def sem(name):
            return stack.enter_context(nc.semaphore(name))

        psum = stack.enter_context(nc.psum_tensor("psum", [P, 8, N_BANK], F32))
        resid = sb("resid", [P, TT, D])
        wkv_hi = sb("wkv_hi", [P, DC, 4 * DH], F32R)
        with ExitStack() as same:
            wkv_sb = same.enter_context(nc.sbuf_tensor("wkv_sb", [P, DC, 4, DH], F32))
        wkv_lo = sb("wkv_lo", [P, DC, 4 * DH], F32R)
        ident = sb("ident", [P, P])
        blockmask = sb("blockmask", [P, P + 4])
        bn6 = sb("bn6", [P, TT, 6])
        mv = sb("mv", [P, TT, 2])
        rstd = sb("rstd", [P, TT])
        std = sb("std", [P, TT])
        kstat = sb("kstat", [P, 3, NG])
        kext = sb("kext", [P, B, 3])
        kbox = sb("kbox", [P, B, 4])
        kbox4 = sb("kbox4", [P, B, 4])
        boxw = sb("boxw", [P, B, 2, DH + 4])
        gap = sb("gap", [P, B])
        gap_ok = sb("gap_ok", [P, 2])
        go_general = sb("go_general", [P, 2], I32)
        kabs = sb("kabs", [P, B])
        kpow = sb("kpow", [P, B])
        kinv = sb("kinv", [P, B])
        qpow = sb("qpow", [P, B])
        vpow = sb("vpow", [P, B])
        rowmax = sb("rowmax", [P, UNITS, LT, 4])
        ones = sb("ones", [P, 2])
        shiftc = sb("shiftc", [P, UNITS * LT])
        shift_hi = sb("shift_hi", [P, P], F16)
        shift_lo = sb("shift_lo", [P, P], F16)
        warm = sb("warm", [P, 2])
        zeros = sb("zeros", [DH, P], F16)

        with ExitStack() as same:
            arena = same.enter_context(nc.sbuf_tensor("arena", [P, 176 * 256 + 64], F32))

        def parts_of_arena(prefix, blocks, holder):
            made, at = {}, 0
            for kib, size in list(blocks.items()) + [(176.25, 0)]:
                if kib > at:
                    holder.enter_context(nc.sbuf_tensor("%s_gap%d" % (prefix, at), [P, int((kib - at) * 256)], F32))
                if size:
                    made[kib] = holder.enter_context(nc.sbuf_tensor("%s_%d" % (prefix, kib), [P, size * 256], F32R))
                at = kib + size
            return made

        with ExitStack() as same:
            context_parts = parts_of_arena("context_parts", {48: 8, 56: 8, 64: 16, 128: 16, 160.25: 16}, same)
        late_parts = parts_of_arena("late_parts", {0: 8, 8: 8, 16: 8, 24: 8, 32: 8, 40: 8, 48: 8, 56: 16, 72: 8, 80: 8, 88: 8,
                                                   96: 8, 104: 8, 112: 8, 120: 8, 128: 8, 146: 8, 160.25: 16}, stack)

        def region(kib, shape, dt=F32):
            n = 1
            for s in shape:
                n *= s
            size = 4 if dt == F32 else 2
            a = arena[:, int(kib * 256):int(kib * 256) + n * size // 4]
            if size == 2:
                a = a.bitcast(dt)
            names = "abcd"[:len(shape)]
            if len(shape) == 1:
                return a
            return a.rearrange("p (%s) -> p %s" % (" ".join(names), " ".join(names)), **dict(zip(names, shape)))

        def chunks(part, n):
            return part[:].rearrange("p (a n) -> p a n", a=n)

        kparts = region(0, [B * M], F16)
        kvT = region(32, [B * M])
        vT = [region(16, [GB // 4, N_BANK]), region(136.25, [GB // 4, N_BANK])]
        ctx_ring = region(96, [4, 4, D])
        ctxT_hi = context_parts[128][:].rearrange("p (s c n) -> p s c n", s=2, c=DC)
        ctxT_lo = context_parts[160.25][:].rearrange("p (s c n) -> p s c n", s=2, c=DC)
        xnorm = region(32, [TT, D])
        wq_sb = region(48, [DC, D])
        wq_lo, wq_hi = chunks(context_parts[48], DC), chunks(context_parts[56], DC)
        x_lo, x_hi = chunks(context_parts[64], DC), chunks(context_parts[160.25], DC)
        qT = region(144.25, [2 * DC, N_BANK])
        qparts = region(32, [UNITS, L], F16)
        prob = region(64, [NP, 2 * N_BANK])
        prob_lo = region(160.25, [NP, 2 * N_BANK], BF16)
        qhi = region(112.25, [2 * DC, N_BANK], F16)
        v_sb = region(96, [B * KT, OC], F16)
        sums = region(112.25, [UNITS, LT, OC])
        sum_rec = region(96, [UNITS, LT])
        heads = region(64, [TT, D])
        qlo = region(120.25, [2 * DC, N_BANK], F16)
        wc_sb = region(146, [DC, D])
        qpos = region(160.25, [DC, N_BANK])
        qneg = region(168.25, [DC, N_BANK])
        box_hi = [region(128.25, [DC, N_BANK], F16), region(144.25, [DC, N_BANK], F16)]
        box_lo = [region(132.25, [DC, N_BANK], F16), region(148.25, [DC, N_BANK], F16)]
        wc_lo, wc_hi = chunks(late_parts[146], DC), chunks(late_parts[32], DC)
        heads_lo = [chunks(late_parts[40], DC), chunks(late_parts[48], DC)]
        wqkv_sb = [region(8 * i, [DC, D]) for i in range(3)]
        wqkv_lo = [chunks(late_parts[8 * i], DC) for i in range(3)]
        wqkv_hi = [chunks(late_parts[32 + 8 * i], DC) for i in range(3)]
        wproj_sb = region(24, [DC, D])
        wproj_lo = chunks(late_parts[24], DC)
        wproj_hi = chunks(late_parts[72], DC)
        feat_hi = chunks(late_parts[160.25], DC)
        feat_lo = chunks(late_parts[56], DC)
        wu_at, wv_at, wo_at = (0, 8), (32, 40), (16, 48)

        def experts_of(part):
            return part[:].rearrange("p (e c r) -> p e c r", e=E // 2, c=DC)

        wu_sb, wv_sb = ([region(k, [E // 2, DC, R]) for k in at] for at in (wu_at, wv_at))
        wu_lo, wv_lo = ([experts_of(late_parts[k]) for k in at] for at in (wu_at, wv_at))
        wu_hi, wv_hi = ([experts_of(late_parts[k]) for k in at] for at in ((80, 88), (96, 104)))
        wo_sb = [region(k, [E // 2, D]) for k in wo_at]
        wo_lo = [chunks(late_parts[k], E // 2) for k in wo_at]
        wo_hi = [chunks(late_parts[k], E // 2) for k in (112, 120)]
        xn2 = region(144, [TT, D])
        qf = region(80, [DC, B * L])
        kf = region(96, [TT, D])
        vf = region(112, [TT, DC, P + 1])
        bias_kv = region(129, [2 * D])
        state = region(133, [B * DC, P + 4])
        ela = region(138, [2, N_BANK])
        elb = region(142, [1, N_BANK])
        la = region(144, [TT, D])
        bproj_sb = sb("bproj_sb", [P, D])
        bq_sb = sb("bq_sb", [P, DC])
        gate_sb = sb("gate_sb", [P, DC, E])
        gate_hi = sb("gate_hi", [P, DC, E], F32R)
        gate_lo = sb("gate_lo", [P, DC, E], F32R)
        lg_rows = region(145, [B, N_BANK])
        lg = sb("lg", [P, TT, E])
        gate = sb("gate", [P, TT, E])
        gmax = sb("gmax", [P, TT])
        gsum = sb("gsum", [P, TT])
        ge = sb("ge", [P, TT, E])
        cmpa = region(24, [TT * E, E])
        cmpb = region(26, [TT * E, E])
        lower = sb("lower", [P, E, E])
        rank = sb("rank", [P, TT, E])
        zden = sb("zden", [P, 2, 2, 4])
        ffe = region(137, [2, N_BANK])
        fft = region(141, [2, N_BANK])
        ffs = late_parts[128][:].rearrange("p (h s n) -> p h s n", h=2, s=2)
        ffs_hi, ffs_lo = ffs[:, 0], ffs[:, 1]

        q_banks = (0, 1, 6, 7)

        names = """x_loaded0 x_loaded1 wq_loaded wkv_loaded ctx_loaded0 ctx_loaded1 ctx_loaded2 ctx_loaded3 consts_ready
            dve_link exp_table_loaded bn_done std_done xn_ready xT_tp xT_copied q_mm q_copied
            ctx_tp ctxT_copied ctxT_split wkv_split ext_ready key_hi unit_rows kv_mm kv_copied stat_done kparts_ready v_scaled q_ready qparts_loaded0 qparts_loaded1 wc_loaded v_tp v_hi v_copied
            max_scores max_read shift_cols shift_tp shift_ready shift_loaded shift_final q_hi qpos_ready qneg_ready box_mm box_hi_ready box_ready box_read box_loaded gap_ready gap_count flag_ready
            scores_ready exp_done lo_ready prob_slot_free out_slot_free heads_ready sums_done
            late_loaded wc_high wc_split concat_tp concat_copied concat_split concat_mm concat_added ffnw_loaded bias_loaded
            qkv_q qkv_qexp qkv_qdone qkv_k qkv_kb qkv_kexp qkv_kdone qkv_v qkv_vdone state_mm state_done
            la_mm la_done la_tp la_copied proj_mm proj_added
            xT_split wq_high wq_split wqkv_high wqkv_split wproj_high wproj_split ffnw_high ffnw_split la_split
            gate_high gate_split logit_rows logit_rows_copied logit_tp logit_read logit_done gate_exp ffn_u ffn_v ffn_sigmoid ffn_s ffn_s_hi ffn_s_split ffn_y ffn_added out_done""".split()
        s = {n: sem(n) for n in names}
        wq_loaded, wkv_loaded, consts_ready = (s[n] for n in ("wq_loaded", "wkv_loaded", "consts_ready"))
        ctx_loaded = [s[f"ctx_loaded{i}"] for i in range(4)]

        x_dram = x.rearrange("b (t p) d -> p (b t) d", p=P)
        out_dram = out.rearrange("b (t p) d -> p (b t) d", p=P)
        ctx_dram = ctx_in.rearrange("b m d -> (b m) d").rearrange("(g t p) d -> g p t d", p=P, t=4)

        block = stack.enter_context(nc.Block())

        @block.sync
        def _(sp):
            def load(dst, src, signal):
                return sp.dma_start(dst, src).then_inc(signal, 16)

            for b in range(B):
                load(resid[:, b * LT:(b + 1) * LT], x_dram[:, b * LT:(b + 1) * LT], s[f"x_loaded{b}"])
            load(wq_sb, w_q.rearrange("(c p) n -> p c n", p=P), wq_loaded)
            for c in range(4):
                load(ctx_ring[:, c], ctx_dram[c], ctx_loaded[c])
                if c == 0:
                    for i in range(4):
                        lo = 0 if i < 3 else DH
                        load(wkv_sb[:, :, i, :], w_kv.rearrange("(c p) n -> p c n", p=P)[:, :, lo:lo + DH], wkv_loaded)
            with sp.Fori(1, NG // 4) as i:
                for c in range(4):
                    sp.wait_ge(s["ctx_tp"], i * 8 + (2 * c - 6))
                    load(ctx_ring[:, c], ctx_dram[bass.ds(4 * i + c, 1)].rearrange("g p t d -> p (g t) d"), ctx_loaded[c])
            qv = qparts.rearrange("p (c j) l -> p c j l", j=4)
            sp.wait_ge(s["v_tp"], KT // 16)
            sp.wait_ge(s["kparts_ready"], 1)
            for b in range(B):
                sp.wait_ge(s["q_ready"], b + 1)
                cs = slice(b * DC, (b + 1) * DC)
                for j in range(4):
                    rows = slice(DH * j, DH * (j + 1))
                    load(qv[0:DH, cs, j, :], qhi[rows, cs, :], s[f"qparts_loaded{b}"])
                    load(qv[DH:2 * DH, cs, j, :], qhi[rows, cs, :], s[f"qparts_loaded{b}"])
                    load(qv[2 * DH:3 * DH, cs, j, :], qlo[rows, cs, :], s[f"qparts_loaded{b}"])
            for b in range(B):
                sp.wait_ge(s["box_ready"], b + 1)
                for c in range(DC):
                    load(qv[3 * DH:3 * DH + 1, b * DC + c], box_hi[b][0:4, c], s["box_loaded"])
                    load(qv[3 * DH + 1:3 * DH + 2, b * DC + c], box_lo[b][0:4, c], s["box_loaded"])
            sp.wait_ge(s["box_loaded"], 32 * B * DC)
            sp.wait_ge(s["flag_ready"], 1)
            with sp.If(sp.value_load(go_general[0:1, 0:1], min_val=0, max_val=1) > 0):
                sp.wait_ge(s["shift_ready"], 2)
                load(qparts[3 * DH:3 * DH + 1].rearrange("p u (t q) -> p (u t) q", q=P), shift_hi[:], s["shift_loaded"])
                load(qparts[3 * DH + 1:3 * DH + 2].rearrange("p u (t q) -> p (u t) q", q=P), shift_lo[:], s["shift_loaded"])
                sp.wait_ge(s["shift_loaded"], 32)
            sp.sem_inc(s["shift_final"], 1)
            sp.wait_ge(s["q_ready"], B)
            sp.wait_ge(s["qpos_ready"], B)
            sp.wait_ge(s["qneg_ready"], B)
            load(wc_sb, w_concat.rearrange("(c p) n -> p c n", p=P), s["wc_loaded"])
            load(bproj_sb[:], b_proj.rearrange("(a n) -> a n", a=1).broadcast_to([P, D]), s["bias_loaded"])
            sp.dma_start(bq_sb[:], b_qkv[0:D].rearrange("(c p) -> p c", p=P), allow_slow_non_contiguous=True)\
                .then_inc(s["bias_loaded"], 16)
            load(gate_sb[:], gate_w.rearrange("(c p) e -> p c e", p=P), s["bias_loaded"])
            sp.wait_ge(s["heads_ready"], TT)
            for i in range(3):
                load(wqkv_sb[i], w_qkv.rearrange("(c p) n -> p c n", p=P)[:, :, i * D:(i + 1) * D], s["late_loaded"])
            load(wproj_sb, w_proj.rearrange("(c p) n -> p c n", p=P), s["late_loaded"])
            sp.wait_ge(s["concat_tp"], TT)
            load(bias_kv, b_qkv[D:3 * D].rearrange("(a n) -> a n", a=1).broadcast_to([P, 2 * D]), s["bias_loaded"])
            sp.wait_ge(s["qkv_q"], 2 * DC)
            sp.wait_ge(s["qkv_k"], TT)
            sp.wait_ge(s["qkv_v"], TT)
            for e in range(E):
                load(wu_sb[e * 2 // E][:, e % (E // 2)], w_u[e].rearrange("(c p) r -> p c r", p=P), s["ffnw_loaded"])
                load(wv_sb[e * 2 // E][:, e % (E // 2)], w_v[e].rearrange("(c p) r -> p c r", p=P), s["ffnw_loaded"])
            for half in range(2):
                load(wo_sb[half], w_o[half * E // 2:(half + 1) * E // 2].rearrange("e r d -> r e d"), s["ffnw_loaded"])
            for t in range(TT):
                sp.wait_ge(s["ffn_added"], (E - 1) * TT + t + 1)
                load(out_dram[:, t], resid[:, t], s["out_done"])
            sp.wait_ge(s["out_done"], 16 * TT)

        @block.gpsimd
        def _(pool):
            done = [0]

            def step(ins):
                done[0] += 1
                ins.then_inc(consts_ready, 1)
                pool.wait_ge(consts_ready, done[0])

            step(nc.gpsimd.memset(ident[:], 0.0))
            step(nc.gpsimd.affine_select(out=ident[:], in_=ident[:], compare_op=ALU.not_equal, fill=1.0, base=0,
                                         pattern=[[-1, P]], channel_multiplier=1))
            step(nc.gpsimd.memset(kparts[3 * DH:3 * DH + 2, 0:M], SHIFT_UNIT))
            step(nc.gpsimd.memset(ones[:], 1.0))
            step(nc.gpsimd.memset(zeros[:], 0.0))
            step(nc.gpsimd.memset(boxw[:], 0.0))
            step(nc.gpsimd.memset(blockmask[:], 0.0))
            for j in range(4):
                rows = slice(DH * j, DH * (j + 1))
                step(nc.gpsimd.memset(blockmask[rows, DH * j:DH * (j + 1)], 1.0))
                step(nc.gpsimd.memset(blockmask[rows, P + j:P + j + 1], 1.0))
            step(nc.gpsimd.memset(lower[:], 0.0))
            for e in range(1, E):
                step(nc.gpsimd.memset(lower[:, e, 0:e], 1.0))
            assert done[0] == CONSTS
            pool.wait_ge(s["v_tp"], KT // 16)
            nc.gpsimd.memset(kparts[3 * DH:3 * DH + 2, M:2 * M], SHIFT_UNIT).then_inc(s["unit_rows"], 1)

        @block.scalar
        def _(act):
            def layernorm_std(k):
                act.wait_ge(s["bn_done"], k + 1)
                nc.scalar.activation(std[:], mv[:, :, 1], ACT.Sqrt).then_inc(s["std_done"], 1)

            layernorm_std(0)
            act.wait_ge(wq_loaded, 16)
            nc.scalar.copy(wq_hi, wq_sb).then_inc(s["wq_high"], 1)
            for i in range(2 * DC):
                b, c = divmod(i, DC)
                act.wait_ge(s["xT_tp"], i + 1)
                nc.scalar.copy(x_hi[:, c, b * L:(b + 1) * L], psum[:, i, :]).then_inc(s["xT_copied"], 1)
            for i in range(2 * DC):
                act.wait_ge(s["q_mm"], i + 1)
                nc.scalar.copy(qT[:, i], psum[:, i, :]).then_inc(s["q_copied"], 1)
            def copy_context(c, group):
                for half in range(2):
                    act.wait_ge(s["ctx_tp"], group * 2 + (half + 1))
                    if half == 0:
                        act.wait_ge(s["kv_mm"], group + 1)
                    nc.scalar.copy(ctxT_hi[:, c % 2, 2 * half:2 * half + 2, :],
                                   psum[:, 2 * half:2 * half + 2, :]).then_inc(s["ctxT_copied"], 1)

            def copy_keys(c, group):
                act.wait_ge(s["kv_mm"], group + 3)
                nc.scalar.activation(kvT[:, bass.ds(group * N_BANK, N_BANK)], psum[:, 4 + c % 2, :], ACT.Copy,
                                     accum_out=kstat[:, 2, bass.ds(group, 1)]).then_inc(s["kv_copied"], 1)

            def some(start, size):
                return slice(start, start + size) if isinstance(start, int) else bass.ds(start, size)

            def scale_keys(b, start, size):
                keys = some(start, size)
                nc.scalar.activation(kparts[0:3 * DH, keys], kvT[0:3 * DH, keys], ACT.Copy,
                                     scale=kinv[0:3 * DH, b:b + 1]).then_inc(s["key_hi"], 1)

            def scale_values(i, j):
                keys = slice((4 * i + j) * N_BANK, (4 * i + j + 1) * N_BANK) if isinstance(i, int) else \
                    bass.ds(i * (4 * N_BANK) + j * N_BANK, N_BANK)
                turn = slice(i, i + 1) if isinstance(i, int) else bass.ds(i, 1)
                nc.scalar.activation(vT[0][DH * j:DH * (j + 1), turn].rearrange("p i n -> p (i n)"), kvT[3 * DH:4 * DH, keys],
                                     ACT.Copy, scale=kinv[3 * DH:4 * DH, 0:1]).then_inc(s["v_scaled"], 1)

            for c in range(4):
                copy_context(c, c)
                if c:
                    copy_keys(c - 1, c - 1)
            with act.Fori(1, GB // 4) as i:
                for c in range(4):
                    copy_context(c, i * 4 + c)
                    copy_keys((c - 1) % 4, i * 4 + (c - 1))
            for c in range(4):
                copy_context(c, GB + c)
                copy_keys((c - 1) % 4, GB + c - 1)
                if c:
                    act.wait_ge(s["ext_ready"], 1)
                    scale_keys(0, (c - 1) * N_BANK, N_BANK)
                    scale_values(0, c - 1)
            with act.Fori(GB // 4 + 1, NG // 4) as i:
                for c in range(4):
                    copy_context(c, i * 4 + c)
                    copy_keys((c - 1) % 4, i * 4 + (c - 1))
                    scale_keys(0, i * (4 * N_BANK) + (c - 1 - GB) * N_BANK, N_BANK)
                    scale_values(i - (GB // 4 + (c == 0)), (c - 1) % 4)
            copy_keys(3, NG - 1)
            scale_keys(0, (GB - 1) * N_BANK, N_BANK)
            scale_values(GB // 4 - 1, 3)

            def queries_above(b):
                if b:
                    act.wait_ge(s["box_mm"], b * DC)
                nc.scalar.activation(qpos, qT[:, b * DC:(b + 1) * DC], ACT.Relu, scale=qpow[:, b:b + 1])\
                    .then_inc(s["qpos_ready"], 1)

            def queries_high(b):
                cs = slice(b * DC, (b + 1) * DC)
                nc.scalar.activation(qhi[:, cs], qT[:, cs], ACT.Copy, scale=qpow[:, b:b + 1]).then_inc(s["q_hi"], 1)

            def values_high(i):
                act.wait_ge(s["v_tp"], i + 1)
                nc.scalar.copy(v_sb[:, 16 * i:16 * (i + 1), 0:DH].rearrange("p (j t) d -> p j t d", j=4),
                               psum[:, (i + 4) % 8, :].rearrange("p (t j d) -> p j t d", t=4, j=4)).then_inc(s["v_hi"], 1)

            def bound_high(b):
                act.wait_ge(s["box_mm"], (b + 1) * DC)
                if b:
                    act.wait_ge(s["q_ready"], 1)
                nc.scalar.copy(box_hi[b][0:4], psum[0:4, b * DC:(b + 1) * DC, :]).then_inc(s["box_hi_ready"], 1)

            act.wait_ge(s["ext_ready"], 1)
            queries_above(0)
            queries_high(0)
            for i in range(KT // 16):
                values_high(i)
            act.wait_ge(s["ext_ready"], 2)
            queries_high(1)
            scale_keys(1, M + M // 2, M // 2)
            queries_above(1)
            bound_high(0)
            scale_keys(1, M, M // 2)
            groups = kvT[3 * DH:4 * DH, M:2 * M].rearrange("p (i j n) -> p i j n", j=4, n=N_BANK)
            for j in range(4):
                nc.scalar.activation(vT[1][DH * j:DH * (j + 1)], groups[:, :, j], ACT.Copy,
                                     scale=kinv[3 * DH:4 * DH, 1:2]).then_inc(s["v_scaled"], 1)
            bound_high(1)
            for i in range(KT // 16, B * KT // 16):
                values_high(i)
            act.wait_ge(consts_ready, CONSTS)
            nc.scalar.activation(warm[:, 0:1], ident[:, 0:1], ACT.Exp).then_inc(s["exp_table_loaded"], 1)
            def exp_round(step0):
                for j in range(NP):
                    act.wait_ge(s["scores_ready"], step0 + (j + 1))
                    act.wait_ge(s["prob_slot_free"], step0 + (j + 1))
                    sl = 2 * (j % 2)
                    nc.scalar.activation(prob[:, j], psum[:, sl:sl + 2, :].rearrange("p a n -> p (a n)"),
                                         ACT.Exp, scale=SCALE).then_inc(s["exp_done"], 1)

            def copy_sums(u, slot):
                act.wait_ge(s["prob_slot_free"], u * STEPS + (STEPS + NP))
                nc.scalar.copy(sums[:, bass.ds(u, 1)].rearrange("p u t c -> p (u t c)"),
                               psum[:, 4 + slot, 0:LT * OC]).then_inc(s["out_slot_free"], 1)

            def exp_unit(u, before=None):
                exp_round(u * STEPS)
                if before is not None:
                    copy_sums(*before)
                with act.Fori(1, STEPS // NP) as i:
                    exp_round(i * NP + u * STEPS)

            exp_unit(0)
            exp_unit(1, (0, 0))
            with act.Fori(1, UNITS // 2) as pair:
                exp_unit(pair * 2, (pair * 2 - 1, 1))
                exp_unit(pair * 2 + 1, (pair * 2, 0))
            act.wait_ge(s["wc_loaded"], 16)
            nc.scalar.copy(wc_hi, wc_sb).then_inc(s["wc_high"], 1)
            copy_sums(UNITS - 1, 1)
            for i in range(TT):
                act.wait_ge(s["concat_tp"], i + 1)
                nc.scalar.activation(feat_hi[:, :, i * P:(i + 1) * P],
                                     psum[:, i % 2, :].rearrange("p (c q) -> p c q", c=DC), ACT.Copy,
                                     scale=vpow[:, i // LT:i // LT + 1]).then_inc(s["concat_copied"], 1)
            act.wait_ge(s["late_loaded"], 64)
            nc.scalar.copy(wproj_hi, wproj_sb).then_inc(s["wproj_high"], 1)
            act.wait_ge(s["bias_loaded"], 64)
            nc.scalar.copy(gate_hi[:], gate_sb[:]).then_inc(s["gate_high"], 1)
            layernorm_std(1)
            act.wait_ge(s["concat_mm"], TT)
            nc.scalar.copy(wqkv_hi[0], wqkv_sb[0]).then_inc(s["wqkv_high"], 1)
            for i in range(2 * DC):
                b, c = divmod(i, DC)
                act.wait_ge(s["xT_tp"], 2 * DC + i + 1)
                nc.scalar.copy(feat_hi[:, c, b * L:(b + 1) * L], psum[:, i, :]).then_inc(s["xT_copied"], 1)
            for part in (1, 2):
                nc.scalar.copy(wqkv_hi[part], wqkv_sb[part]).then_inc(s["wqkv_high"], 1)
            act.wait_ge(s["bias_loaded"], 64)
            for i in range(2 * DC):
                b, c = divmod(i, DC)
                act.wait_ge(s["qkv_q"], i + 1)
                if i >= 2:
                    act.wait_ge(s["qkv_qdone"], i - 1)
                nc.scalar.activation(ela[:, i % 2], psum[:, q_banks[i % 4], :], ACT.Exp,
                                     bias=bq_sb[:, c:c + 1]).then_inc(s["qkv_qexp"], 1)
            for t in range(TT):
                act.wait_ge(s["qkv_kb"], t + 1)
                if t == 0:
                    act.wait_ge(s["qkv_qdone"], 2 * DC)
                else:
                    act.wait_ge(s["qkv_kdone"], max(t - 1, 1))
                nc.scalar.activation(ela[:, t % 2], kf[:, t], ACT.Exp).then_inc(s["qkv_kexp"], 1)
            def expert_high(k):
                if k == 0:
                    act.wait_ge(s["la_mm"], TT)
                    act.wait_ge(s["ffnw_loaded"], 16 * (2 * E + 2))
                half, e = divmod(k, E // 2)
                for high, loaded in ((wu_hi, wu_sb), (wv_hi, wv_sb), (wo_hi, wo_sb)):
                    nc.scalar.copy(high[half][:, e], loaded[half][:, e]).then_inc(s["ffnw_high"], 1)

            for i in range(TT):
                act.wait_ge(s["la_tp"], i + 1)
                nc.scalar.copy(feat_hi[:, :, i * P:(i + 1) * P],
                               psum[:, 4 + i % 2, :].rearrange("p (c q) -> p c q", c=DC)).then_inc(s["la_copied"], 1)
                if 2 <= i < E:
                    expert_high(i - 2)
            expert_high(E - 2)
            expert_high(E - 1)
            layernorm_std(2)
            for i in range(2 * DC):
                b, c = divmod(i, DC)
                act.wait_ge(s["xT_tp"], 4 * DC + i + 1)
                nc.scalar.copy(feat_hi[:, c, b * L:(b + 1) * L], psum[:, i, :]).then_inc(s["xT_copied"], 1)
            for b in range(B):
                act.wait_ge(s["logit_rows"], b + 1)
                nc.scalar.copy(lg_rows[0:E, b], psum[0:E, 6 + b, :]).then_inc(s["logit_rows_copied"], 1)
            def products_high(i):
                act.wait_ge(s["ffn_s"], i + 1)
                if i >= 2:
                    act.wait_ge(s["ffn_y"], (i - 1) * LT)
                nc.scalar.copy(ffs_hi[:, i % 2], fft[:, i % 2]).then_inc(s["ffn_s_hi"], 1)

            def sigmoid(i):
                act.wait_ge(s["ffn_u"], i + 1)
                if i >= 2:
                    act.wait_ge(s["ffn_s"], i - 1)
                nc.scalar.activation(ffe[:, i % 2], psum[:, i % 2, :], ACT.Sigmoid).then_inc(s["ffn_sigmoid"], 1)

            sigmoid(0)
            products_high(0)
            act.wait_ge(s["logit_done"], 1)
            nc.scalar.activation(ge[:], lg[:], ACT.Exp).then_inc(s["gate_exp"], 1)
            for i in range(1, E * B):
                sigmoid(i)
                if i >= 2:
                    products_high(i - 1)
            products_high(E * B - 1)

        @block.vector
        def _(dve):
            n = [0]

            def link(ins):
                n[0] += 1
                ins.then_inc(s["dve_link"], 1)
                dve.wait_ge(s["dve_link"], n[0])

            def statistics(t):
                return nc.vector.bn_stats(bn6[:, t], resid[:, t])

            def layernorm(k, dst):
                link(statistics(TT - 1))
                for t in range(TT):
                    last = nc.vector.bn_aggr(mv[:, t], bn6[:, t])
                link(last)
                nc.vector.tensor_scalar(mv[:, :, 1], mv[:, :, 1], EPS_LN, None, ALU.add).then_inc(s["bn_done"], 1)
                dve.wait_ge(s["std_done"], k + 1)
                link(nc.vector.reciprocal(rstd[:], std[:]))
                for t in range(TT):
                    nc.vector.tensor_scalar(dst[:, t], resid[:, t], mv[:, t, 0:1], rstd[:, t:t + 1],
                                            ALU.subtract, ALU.mult).then_inc(s["xn_ready"], 1)

            for t in range(TT - 1):
                if t % LT == 0:
                    dve.wait_ge(s[f"x_loaded{t // LT}"], 16)
                statistics(t)
            layernorm(0, xnorm)

            def low_part(dst, src, high):
                return nc.vector.tensor_tensor(dst, src, high.bitcast(F32), ALU.subtract)

            def split_tokens(k, low, high):
                for i in range(2 * DC):
                    b, c = divmod(i, DC)
                    cols = slice(b * L, (b + 1) * L)
                    dve.wait_ge(s["xT_copied"], 2 * DC * k + i + 1)
                    low_part(low[:, c, cols], psum[:, i, :], high[:, c, cols]).then_inc(s["xT_split"], 1)

            dve.wait_ge(s["wq_high"], 1)
            low_part(wq_lo, wq_sb, wq_hi).then_inc(s["wq_split"], 1)
            split_tokens(0, x_lo, x_hi)
            dve.wait_ge(wkv_loaded, 64)
            wkv_flat = wkv_sb[:].rearrange("p c a n -> p c (a n)")
            link(nc.vector.tensor_copy(wkv_hi[:], wkv_flat))
            nc.vector.tensor_tensor(wkv_lo[:], wkv_flat, wkv_hi[:].bitcast(F32), ALU.subtract).then_inc(s["wkv_split"], 1)

            def split_context(c, group):
                for half in range(2):
                    dve.wait_ge(s["ctxT_copied"], group * 2 + (half + 1))
                    fs = slice(2 * half, 2 * half + 2)
                    nc.vector.tensor_tensor(ctxT_lo[:, c % 2, fs, :], psum[:, fs, :], ctxT_hi[:, c % 2, fs, :].bitcast(F32),
                                            ALU.subtract).then_inc(s["ctxT_split"], 1)

            def extremes(group):
                dve.wait_ge(s["kv_copied"], group + 1)
                src = kvT[:, bass.ds(group * N_BANK, N_BANK)]
                nc.vector.tensor_reduce(kstat[:, 0, bass.ds(group, 1)], src, AX, ALU.max)
                nc.vector.tensor_reduce(kstat[:, 1, bass.ds(group, 1)], src, AX, ALU.min).then_inc(s["stat_done"], 1)

            def key_low(b, start, size, count):
                dve.wait_ge(s["key_hi"], count)
                keys = slice(start, start + size) if isinstance(start, int) else bass.ds(start, size)
                return nc.vector.scalar_tensor_tensor(kparts[DH:2 * DH, keys], kvT[DH:2 * DH, keys],
                                                      kinv[DH:2 * DH, b:b + 1], kparts[DH:2 * DH, keys],
                                                      ALU.mult, ALU.subtract)

            def box_of_keys(b):
                dve.wait_ge(s["stat_done"], GB * (b + 1))
                gs = slice(b * GB, (b + 1) * GB)
                nc.vector.tensor_reduce(kext[:, b, 0:1], kstat[:, 0, gs], AX, ALU.max)
                nc.vector.tensor_reduce(kext[:, b, 2:3], kstat[:, 2, gs], AX, ALU.add)
                link(nc.vector.tensor_reduce(kext[:, b, 1:2], kstat[:, 1, gs], AX, ALU.min))
                bb = slice(b, b + 1)
                link(nc.vector.scalar_tensor_tensor(kabs[:, bb], kext[:, b, 1:2], -1.0, kext[:, b, 0:1],
                                                    ALU.mult, ALU.max))
                link(nc.vector.tensor_scalar(kabs[:, bb], kabs[:, bb], 1e-30, None, ALU.max))
                link(nc.vector.tensor_scalar(kpow[:, bb].bitcast(I32), kabs[:, bb].bitcast(I32), EXPONENT_BITS, None,
                                             ALU.bitwise_and))
                link(nc.vector.reciprocal(kinv[:, bb], kpow[:, bb]))
                for j in range(4):
                    rows = slice(DH * j, DH * (j + 1))
                    nc.vector.tensor_copy(qpow[rows, bb], kpow[0:DH, bb])
                    last = nc.vector.tensor_copy(vpow[rows, bb], kpow[3 * DH:4 * DH, bb])
                link(last)
                link(nc.vector.tensor_scalar(kext[:, b, 2:3], kext[:, b, 2:3], 1.0 / M, None, ALU.mult))
                link(nc.vector.tensor_scalar(kext[:, b], kext[:, b], kinv[:, bb], None, ALU.mult))
                nc.vector.tensor_scalar(kbox[:, b, 0:1], kext[:, b, 0:1], -1.0 / SHIFT_UNIT, None, ALU.mult)
                nc.vector.tensor_tensor(kbox[:, b, 1:2], kext[:, b, 0:1], kext[:, b, 2:3], ALU.subtract)
                nc.vector.tensor_scalar(kbox[:, b, 2:3], kext[:, b, 1:2], -1.0 / SHIFT_UNIT, None, ALU.mult)
                link(nc.vector.tensor_tensor(kbox[:, b, 3:4], kext[:, b, 1:2], kext[:, b, 2:3], ALU.subtract))
                for j in range(4):
                    last = nc.vector.tensor_copy(kbox4[DH * j:DH * (j + 1), b], kbox[0:DH, b])
                link(last)
                dve.wait_ge(consts_ready, CONSTS)
                for k in range(4):
                    last = nc.vector.tensor_scalar(boxw[:, b, k // 2, DH * (k % 2):DH * (k % 2) + 4], blockmask[:, P:P + 4],
                                                   kbox4[:, b, k:k + 1], None, ALU.mult)
                last.then_inc(s["ext_ready"], 1)
                dve.wait_ge(s["ext_ready"], b + 1)

            def queries_below(b):
                if b:
                    dve.wait_ge(s["box_mm"], b * DC)
                nc.vector.tensor_scalar(qneg, qT[:, b * DC:(b + 1) * DC], qpow[:, b:b + 1], 0.0, ALU.mult, ALU.min)\
                    .then_inc(s["qneg_ready"], 1)

            split_context(0, 0)
            for c in range(1, 4):
                split_context(c, c)
                extremes(c - 1)
            with dve.Fori(1, GB // 4) as i:
                for c in range(4):
                    split_context(c, i * 4 + c)
                    extremes(i * 4 + (c - 1))
            split_context(0, GB)
            extremes(GB - 1)
            box_of_keys(0)
            for c in range(1, 4):
                split_context(c, GB + c)
                extremes(GB + c - 1)
                key_low(0, (c - 1) * N_BANK, N_BANK, c)
            with dve.Fori(GB // 4 + 1, NG // 4) as i:
                for c in range(4):
                    split_context(c, i * 4 + c)
                    extremes(i * 4 + (c - 1))
                    key_low(0, i * (4 * N_BANK) + (c - 1 - GB) * N_BANK, N_BANK, i * 4 + (c - GB))
            dve.wait_ge(s["kv_copied"], NG)
            dve.wait_ge(s["q_copied"], 2 * DC)
            queries_below(0)
            extremes(NG - 1)
            box_of_keys(1)
            key_low(0, (GB - 1) * N_BANK, N_BANK, GB).then_inc(s["kparts_ready"], 1)

            def queries_low(b):
                cs = slice(b * DC, (b + 1) * DC)
                dve.wait_ge(s["q_hi"], b + 1)
                nc.vector.scalar_tensor_tensor(qlo[:, cs], qT[:, cs], qpow[:, b:b + 1], qhi[:, cs],
                                               ALU.mult, ALU.subtract).then_inc(s["q_ready"], 1)

            def value_low(i):
                dve.wait_ge(s["v_hi"], i + 1)
                tiles = slice(16 * i, 16 * (i + 1))
                v_of = v_sb[:, tiles].rearrange("p (j t) c -> p j t c", j=4)
                nc.vector.tensor_tensor(v_of[:, :, :, DH:2 * DH], psum[:, (i + 4) % 8, :].rearrange("p (t j d) -> p j t d", t=4, j=4),
                                        v_of[:, :, :, 0:DH], ALU.subtract).then_inc(s["v_copied"], 1)

            def bound(b):
                dve.wait_ge(s["box_hi_ready"], b + 1)
                nc.vector.tensor_tensor(box_lo[b][0:4], psum[0:4, b * DC:(b + 1) * DC, :], box_hi[b][0:4], ALU.subtract)\
                    .then_inc(s["box_ready"], 1)
                nc.vector.tensor_reduce(gap[DH:DH + 4, b:b + 1], psum[DH:DH + 4, b * DC:(b + 1) * DC, :].rearrange("p a n -> p (a n)"),
                                        AX, ALU.max).then_inc(s["box_read"], 1)

            queries_low(0)
            nc.vector.memset(v_sb[:, :, 2 * DH:OC], 1.0)
            for i in range(KT // 16):
                value_low(i)
            queries_low(1)
            queries_below(1)
            bound(0)
            key_low(1, M + M // 2, M // 2, GB + 1)
            key_low(1, M, M // 2, GB + 2).then_inc(s["kparts_ready"], 1)
            bound(1)
            dve.wait_ge(s["box_read"], B)
            link(nc.vector.tensor_reduce(gap_ok[DH:DH + 4, 0:1], gap[DH:DH + 4, :], AX, ALU.max))
            nc.vector.tensor_scalar(gap_ok[DH:DH + 4, 1:2], gap_ok[DH:DH + 4, 0:1], GAP_LIMIT / SCALE, None, ALU.is_le)\
                .then_inc(s["gap_ready"], 1)
            dve.wait_ge(s["gap_count"], 1)
            nc.vector.tensor_scalar(go_general[0:1, 0:1], psum[0:1, 4, 0:1], 3.5, None, ALU.is_lt)\
                .then_inc(s["flag_ready"], 1)
            for i in range(KT // 16, B * KT // 16):
                value_low(i)
            dve.wait_ge(s["flag_ready"], 1)
            with dve.If(dve.value_load(go_general[0:1, 0:1], min_val=0, max_val=1) > 0):
                for b in range(B):
                    with dve.Fori(0, H) as h:
                        for t in range(LT):
                            for k in range(4):
                                i0 = b * H * 16 + t * 4 + k
                                dve.wait_ge(s["max_scores"], h * 16 + i0 + 1)
                                sl = 4 * (k % 2)
                                nc.vector.tensor_reduce(rowmax[:, bass.ds(h + b * H, 1), t, k:k + 1],
                                                        psum[:, sl:sl + 4, :].rearrange("p a n -> p (a n)"),
                                                        AX, ALU.max).then_inc(s["max_read"], 1)
                dve.wait_ge(s["max_read"], 2 + UNITS * 16)
                nc.vector.tensor_reduce(shiftc[:], rowmax[:].rearrange("p u t k -> p (u t) k"), AX, ALU.max)\
                    .then_inc(s["shift_cols"], 1)
                dve.wait_ge(s["shift_tp"], 1)
                nc.vector.tensor_scalar(shift_hi[:], psum[:, 0, 0:P], -1.0 / SHIFT_UNIT, None, ALU.mult)\
                    .then_inc(s["shift_ready"], 1)
                dve.wait_ge(s["shift_ready"], 1)
                nc.vector.scalar_tensor_tensor(shift_lo[:], psum[:, 0, 0:P], -1.0 / SHIFT_UNIT, shift_hi[:],
                                               ALU.mult, ALU.subtract).then_inc(s["shift_ready"], 1)


            with dve.Fori(0, UNITS * STEPS // NP) as i:
                for j in range(0, NP, 2):
                    dve.wait_ge(s["exp_done"], i * NP + (j + 4))
                    both = prob[:, j:j + 2].rearrange("p a n -> p (a n)")
                    hi = both.bitcast(BF16).rearrange("p (n two) -> p n two", two=2)[:, :, 1]
                    nc.vector.tensor_tensor(prob_lo[:, j:j + 2].rearrange("p a n -> p (a n)"), both, hi, ALU.subtract)\
                        .then_inc(s["lo_ready"], 1)
            dve.wait_ge(s["wc_high"], 1)
            low_part(wc_lo, wc_sb, wc_hi).then_inc(s["wc_split"], 1)
            def split_heads(t):
                b = t // LT
                dve.wait_ge(s["concat_copied"], t + 1)
                nc.vector.scalar_tensor_tensor(heads_lo[b][:, :, (t % LT) * P:(t % LT + 1) * P],
                                               psum[:, t % 2, :].rearrange("p (c q) -> p c q", c=DC), vpow[:, b:b + 1],
                                               feat_hi[:, :, t * P:(t + 1) * P].bitcast(F32), ALU.mult, ALU.subtract)\
                    .then_inc(s["concat_split"], 1)

            dve.wait_ge(s["out_slot_free"], UNITS + 2)
            for b in range(B):
                us = slice(b * H, (b + 1) * H)
                nc.vector.reciprocal(sum_rec[:, us], sums[:, us, :, 2 * DH]).then_inc(s["sums_done"], 1)
                nc.vector.tensor_tensor(sums[:, us, :, 0:DH], sums[:, us, :, 0:DH], sums[:, us, :, DH:2 * DH], ALU.add)\
                    .then_inc(s["sums_done"], 1)
                dve.wait_ge(s["sums_done"], 2 * (b + 1))
                for t in range(LT):
                    nc.vector.tensor_tensor(heads[:, b * LT + t].rearrange("p (h d) -> p h d", d=DH), sums[:, us, t, 0:DH],
                                            sum_rec[:, us, t:t + 1].broadcast_to([P, H, DH]), ALU.mult)\
                        .then_inc(s["heads_ready"], 1)
                if b == 0:
                    split_heads(0)
                    split_heads(1)

            for t in range(TT):
                if 2 <= t + 1 < TT:
                    split_heads(t + 1)
                dve.wait_ge(s["concat_mm"], t + 1)
                nc.vector.tensor_tensor(resid[:, t], psum[:, 2 + t % 2, :], resid[:, t], ALU.add)\
                    .then_inc(s["concat_added"], 1)
                dve.wait_ge(s["concat_added"], t + 1)
                if t < TT - 1:
                    statistics(t)
            layernorm(1, xn2)

            def split_wqkv(part):
                dve.wait_ge(s["wqkv_high"], part + 1)
                low_part(wqkv_lo[part], wqkv_sb[part], wqkv_hi[part]).then_inc(s["wqkv_split"], 1)

            split_wqkv(0)
            split_tokens(1, feat_lo, feat_hi)

            def between(t):
                if t == 1:
                    dve.wait_ge(s["gate_high"], 1)
                    low_part(gate_lo[:], gate_sb[:], gate_hi[:]).then_inc(s["gate_split"], 1)
                if t == 2:
                    dve.wait_ge(s["wproj_high"], 1)
                    low_part(wproj_lo, wproj_sb, wproj_hi).then_inc(s["wproj_split"], 1)
                link(nc.vector.tensor_tensor(resid[:, t], resid[:, t], bproj_sb[:], ALU.add))

            dve.wait_ge(s["bias_loaded"], 64)
            for i in range(2 * DC):
                b, c = divmod(i, DC)
                dve.wait_ge(s["qkv_qexp"], i + 1)
                link(nc.vector.tensor_scalar(elb[:, 0], psum[:, q_banks[i % 4], :], bq_sb[:, c:c + 1], 0.0, ALU.add, ALU.max))
                nc.vector.scalar_tensor_tensor(qf[:, c, b * L:(b + 1) * L], ela[:, i % 2], 1.0, elb[:, 0],
                                               ALU.min, ALU.add).then_inc(s["qkv_qdone"], 1)
                dve.wait_ge(s["qkv_qdone"], i + 1)
                if i in (1, 3):
                    split_wqkv((i + 1) // 2)
            link(nc.vector.memset(vf[:, :, :, P:P + 1], 1.0))
            for t in range(TT):
                dve.wait_ge(s["qkv_k"], t + 1)
                nc.vector.tensor_tensor(kf[:, t], psum[:, 2 + t % 2, :], bias_kv[:, 0:D], ALU.add).then_inc(s["qkv_kb"], 1)
                dve.wait_ge(s["qkv_v"], t + 1)
                nc.vector.tensor_tensor(vf[:, t, :, 0:P], psum[:, 4 + t % 2, :].rearrange("p (c n) -> p c n", c=DC),
                                        bias_kv[:, D:2 * D].rearrange("p (c n) -> p c n", c=DC), ALU.add)\
                    .then_inc(s["qkv_vdone"], 1)
                dve.wait_ge(s["qkv_kexp"], t + 1)
                link(nc.vector.tensor_scalar(kf[:, t], kf[:, t], 0.0, None, ALU.max))
                nc.vector.scalar_tensor_tensor(kf[:, t], ela[:, t % 2], 1.0, kf[:, t], ALU.min, ALU.add)\
                    .then_inc(s["qkv_kdone"], 1)
                between(t)
            for i in range(2 * DC):
                dve.wait_ge(s["state_mm"], i + 1)
                ps = psum[:, i % 2, :]
                nc.vector.tensor_tensor(state[:, i, 0:P], ps[:, 0:P], blockmask[:, 0:P], ALU.mult)
                nc.vector.tensor_scalar(state[:, i, P:P + 4], blockmask[:, P:P + 4], ps[:, P:P + 1], None, ALU.mult)\
                    .then_inc(s["state_done"], 1)
            for t in range(TT):
                dve.wait_ge(s["la_mm"], t + 1)
                sl = 2 * (t % 2)
                o = psum[:, sl:sl + 2, 0:2 * (P + 4)].rearrange("p a (c n) -> p a c n", c=2)
                link(nc.vector.tensor_scalar(zden[:], o[:, :, :, P:P + 4], EPS_Z, None, ALU.add))
                link(nc.vector.reciprocal(zden[:], zden[:]))
                for a in range(2):
                    last = nc.vector.tensor_tensor(
                        la[:, t, a * 256:(a + 1) * 256].rearrange("p (c j d) -> p c j d", c=2, j=4),
                        o[:, a, :, 0:P].rearrange("p c (j d) -> p c j d", j=4),
                        zden[:, a].rearrange("p c (j o) -> p c j o", o=1).broadcast_to([P, 2, 4, DH]), ALU.mult)
                last.then_inc(s["la_done"], 1)
                dve.wait_ge(s["la_done"], t + 1)
            def add_projection(t):
                dve.wait_ge(s["proj_mm"], t + 1)
                nc.vector.tensor_tensor(resid[:, t], psum[:, 6 + t % 2, :], resid[:, t], ALU.add)\
                    .then_inc(s["proj_added"], 1)

            def split_expert(k):
                dve.wait_ge(s["ffnw_high"], 3 * (k + 1))
                half, e = divmod(k, E // 2)
                for low, loaded, high in ((wu_lo, wu_sb, wu_hi), (wv_lo, wv_sb, wv_hi), (wo_lo, wo_sb, wo_hi)):
                    last = low_part(low[half][:, e], loaded[half][:, e], high[half][:, e])
                last.then_inc(s["ffnw_split"], 1)

            for t in range(TT):
                cols = slice(t * P, (t + 1) * P)
                dve.wait_ge(s["la_copied"], t + 1)
                low_part(feat_lo[:, :, cols], psum[:, 4 + t % 2, :].rearrange("p (c q) -> p c q", c=DC), feat_hi[:, :, cols])\
                    .then_inc(s["la_split"], 1)
                if t:
                    add_projection(t - 1)
                    dve.wait_ge(s["proj_added"], t)
                    statistics(t - 1)
                if 3 <= t <= 4:
                    split_expert(t - 3)
            add_projection(TT - 1)
            dve.wait_ge(s["proj_added"], TT)
            layernorm(2, xn2)
            split_tokens(2, feat_lo, feat_hi)
            def add_experts(i):
                e, b = divmod(i, B)
                for t in range(LT):
                    k = i * LT + t
                    dve.wait_ge(s["ffn_y"], k + 1)
                    tok = b * LT + t
                    if e:
                        dve.wait_ge(s["ffn_added"], k - B * LT + 1)
                    nc.vector.scalar_tensor_tensor(resid[:, tok], psum[:, 4 + k % 4, :], gate[:, tok, e:e + 1],
                                                   resid[:, tok], ALU.mult, ALU.add).then_inc(s["ffn_added"], 1)

            def expert_products(i):
                dve.wait_ge(s["ffn_sigmoid"], i + 1)
                if i >= 2:
                    dve.wait_ge(s["ffn_s_hi"], i - 1)
                link(nc.vector.tensor_tensor(fft[:, i % 2], psum[:, i % 2, :], ffe[:, i % 2], ALU.mult))
                dve.wait_ge(s["ffn_v"], i + 1)
                nc.vector.tensor_tensor(fft[:, i % 2], psum[:, 2 + i % 2, :], fft[:, i % 2], ALU.mult)\
                    .then_inc(s["ffn_s"], 1)
                dve.wait_ge(s["ffn_s_hi"], i + 1)
                low_part(ffs_lo[:, i % 2], fft[:, i % 2], ffs_hi[:, i % 2]).then_inc(s["ffn_s_split"], 1)

            expert_products(0)
            dve.wait_ge(consts_ready, CONSTS)
            dve.wait_ge(s["logit_tp"], 1)
            nc.vector.tensor_copy(lg[:], psum[:, 7, 0:TT * E].rearrange("p (t e) -> p t e", e=E)).then_inc(s["logit_read"], 1)
            dve.wait_ge(s["logit_read"], 1)
            flat = lg[:].rearrange("p t e -> p (t e)")
            for e in range(E):
                le = lg[:, :, e:e + 1].broadcast_to([P, TT, E])
                ca = cmpa.rearrange("p (t e) j -> p t e j", e=E)[:, :, e, :]
                cb = cmpb.rearrange("p (t e) j -> p t e j", e=E)[:, :, e, :]
                nc.vector.tensor_tensor(ca, lg[:], le, ALU.is_gt)
                link(nc.vector.tensor_tensor(cb, lg[:], le, ALU.is_equal))
                link(nc.vector.tensor_tensor(cb, cb, lower[:, e:e + 1, :].broadcast_to([P, TT, E]), ALU.mult))
            link(nc.vector.tensor_tensor(cmpa, cmpa, cmpb, ALU.add))
            link(nc.vector.tensor_reduce(rank[:].rearrange("p t e -> p (t e)"), cmpa, AX, ALU.add))
            link(nc.vector.tensor_scalar(rank[:], rank[:], 1.5, None, ALU.is_lt))
            link(nc.vector.tensor_reduce(gmax[:], lg[:], AX, ALU.max))
            nc.vector.tensor_tensor(lg[:], lg[:], gmax[:].rearrange("p (t o) -> p t o", o=1).broadcast_to([P, TT, E]),
                                    ALU.subtract).then_inc(s["logit_done"], 1)
            dve.wait_ge(s["gate_exp"], 1)
            link(nc.vector.tensor_tensor(gate[:], ge[:], rank[:], ALU.mult))
            link(nc.vector.tensor_reduce(gsum[:], gate[:], AX, ALU.add))
            link(nc.vector.reciprocal(gsum[:], gsum[:]))
            link(nc.vector.tensor_tensor(gate[:], gate[:],
                                         gsum[:].rearrange("p (t o) -> p t o", o=1).broadcast_to([P, TT, E]), ALU.mult))

            for i in range(1, E * B):
                if i % 2 == 1 and 2 <= (i + 3) // 2 < E:
                    split_expert((i + 3) // 2)
                expert_products(i)
                add_experts(i - 1)
            add_experts(E * B - 1)

        @block.tensor
        def _(pe):
            def transpose_tokens(k, src):
                for i in range(2 * DC):
                    b, c = divmod(i, DC)
                    if c == 0:
                        pe.wait_ge(s["xn_ready"], k * TT + (b + 1) * LT)
                    for t in range(LT):
                        last = nc.tensor.transpose(psum[:, i, t * P:(t + 1) * P],
                                                   src[:, b * LT + t, c * P:(c + 1) * P], ident[:])
                    last.then_inc(s["xT_tp"], 1)

            def split_products(dst, left, right, signal):
                pairs = [(left[0](c), right[0](c)) for c in range(DC)] + [(left[0](c), right[1](c)) for c in range(DC)] + \
                    [(left[1](c), right[0](c)) for c in range(DC)]
                for n, (l, r) in enumerate(pairs):
                    last = nc.tensor.matmul(dst, l, r, start=(n == 0), stop=(n == len(pairs) - 1))
                last.then_inc(signal, 1)

            def parts(high, low, cols):
                return lambda c: high[:, c, cols], lambda c: low[:, c, cols]

            pe.wait_ge(consts_ready, 2)
            transpose_tokens(0, xnorm)
            pe.wait_ge(s["wq_split"], 1)
            for i in range(2 * DC):
                b, m = divmod(i, DC)
                if m == 0:
                    pe.wait_ge(s["xT_split"], (b + 1) * DC)
                split_products(psum[:, i, :], parts(wq_hi, wq_lo, slice(m * P, (m + 1) * P)),
                               parts(x_hi, x_lo, slice(b * L, (b + 1) * L)), s["q_mm"])
            pe.wait_ge(s["q_copied"], 2 * DC)
            pe.wait_ge(s["wkv_split"], 1)
            pe.sem_inc(s["kv_mm"], 2)

            def transpose_context(c, loaded, copied):
                pe.wait_ge(ctx_loaded[c], loaded)
                for half in range(2):
                    if copied is not None:
                        pe.wait_ge(s["ctxT_split"], copied + half)
                    for cc in range(2):
                        for t in range(4):
                            f = 2 * half + cc
                            last = nc.tensor.transpose(psum[:, f, t * P:(t + 1) * P],
                                                       ctx_ring[:, c, t, f * P:(f + 1) * P], ident[:])
                    last.then_inc(s["ctx_tp"], 1)

            def multiply_context(c, copied, free):
                pe.wait_ge(s["ctxT_split"], copied)
                if free is not None:
                    pe.wait_ge(s["kv_copied"], free)
                products = [(w, t, f) for f in range(DC) for w, t in ((wkv_hi, ctxT_hi), (wkv_hi, ctxT_lo), (wkv_lo, ctxT_hi))]
                for n, (w, t, f) in enumerate(products):
                    last = nc.tensor.matmul(psum[:, 4 + c % 2, :], w[:, f], t[:, c % 2, f, :],
                                            start=(n == 0), stop=(n == len(products) - 1))
                last.then_inc(s["kv_mm"], 1)

            transpose_context(0, 16, None)
            for c in range(4):
                if c < 3:
                    transpose_context(c + 1, 16, 2 * c + 1)
                else:
                    transpose_context(0, 32, 2 * c + 1)
                multiply_context(c, 2 * c + 2, c - 1 if c >= 2 else None)
            with pe.Fori(1, NG // 4 - 1) as i:
                for c in range(4):
                    if c < 3:
                        transpose_context(c + 1, i * 16 + 16, i * 8 + 2 * c + 1)
                    else:
                        transpose_context(0, i * 16 + 32, i * 8 + 2 * c + 1)
                    multiply_context(c, i * 8 + 2 * c + 2, i * 4 + c - 1)
            last_round = NG // 4 - 1
            for c in range(4):
                if c < 3:
                    transpose_context(c + 1, last_round * 16 + 16, last_round * 8 + 2 * c + 1)
                multiply_context(c, last_round * 8 + 2 * c + 2, last_round * 4 + c - 1)

            def transpose_values(banks):
                for i in banks:
                    b, turn = divmod(i, KT // 16)
                    for t in range(4):
                        last = nc.tensor.transpose(psum[:, (i + 4) % 8, t * P:(t + 1) * P], vT[b][:, turn, t * P:(t + 1) * P],
                                                   ident[:])
                    last.then_inc(s["v_tp"], 1)

            def bound(b):
                pe.wait_ge(s["qneg_ready"], b + 1)
                pe.wait_ge(s["qpos_ready"], b + 1)
                for c in range(DC):
                    nc.tensor.matmul(psum[0:DH + 4, b * DC + c, :], boxw[:, b, 0], qpos[:, c], start=True, stop=False)
                    nc.tensor.matmul(psum[0:DH + 4, b * DC + c, :], boxw[:, b, 1], qneg[:, c], start=False, stop=True)\
                        .then_inc(s["box_mm"], 1)

            pe.wait_ge(s["kv_copied"], NG)
            pe.wait_ge(s["v_scaled"], GB)
            transpose_values(range(KT // 16))
            pe.wait_ge(s["ctxT_split"], 2 * NG)
            bound(0)
            pe.wait_ge(s["v_copied"], KT // 16)
            bound(1)
            pe.wait_ge(s["box_read"], 1)
            pe.wait_ge(s["v_scaled"], GB + 4)
            transpose_values(range(KT // 16, B * KT // 16))
            pe.wait_ge(s["gap_ready"], 1)
            nc.tensor.matmul(psum[0:1, 4, 0:1], gap_ok[DH:DH + 4, 1:2], ones[DH:DH + 4, 0:1], start=True, stop=True)\
                .then_inc(s["gap_count"], 1)
            pe.wait_ge(s["kparts_ready"], B)
            pe.wait_ge(s["unit_rows"], 1)
            pe.wait_ge(s["v_copied"], B * KT // 16)
            pe.wait_ge(s["flag_ready"], 1)
            for b in range(B):
                pe.wait_ge(s[f"qparts_loaded{b}"], 16 * 12)
            with pe.If(pe.value_load(go_general[0:1, 0:1], min_val=0, max_val=1) > 0):
                pe.sem_inc(s["max_read"], 2)
                for b in range(B):
                    with pe.Fori(0, H) as h:
                        for t in range(LT):
                            for k in range(4):
                                pe.wait_ge(s["max_read"], h * 16 + (b * H * 16 + t * 4 + k + 1))
                                for a in range(4):
                                    lhs = qparts[0:3 * DH, bass.ds(h + b * H, 1), t * P:(t + 1) * P]
                                    last = nc.tensor.matmul(psum[:, 4 * (k % 2) + a, :], lhs.rearrange("p u q -> p (u q)"),
                                                            kparts[0:3 * DH, b * M + (4 * k + a) * N_BANK:
                                                                   b * M + (4 * k + a + 1) * N_BANK], start=True, stop=True)
                                last.then_inc(s["max_scores"], 1)
                pe.wait_ge(s["shift_cols"], 1)
                nc.tensor.transpose(psum[:, 0, 0:P], shiftc[:], ident[:]).then_inc(s["shift_tp"], 1)

            pe.wait_ge(s["shift_final"], 1)

            pe.sem_inc(s["exp_done"], 2)
            pe.sem_inc(s["prob_slot_free"], NP)
            pe.sem_inc(s["out_slot_free"], 2)

            def scores(b, h, step, j, count):
                pe.wait_ge(s["exp_done"], count)
                q = qparts[0:3 * DH + 2, bass.ds(h + b * H, 1), :].rearrange("p u q -> p (u q)")
                for a in range(2):
                    keys = kparts[0:3 * DH + 2, bass.ds(step * (2 * P) + (b * M + a * P), P)]
                    last = nc.tensor.matmul(psum[:, 2 * (j % 2) + a, :], keys, q, start=True, stop=True)
                last.then_inc(s["scores_ready"], 1)

            def values(b, step, j, pairs_done, slot, last_step):
                if j % 2 == 0:
                    pe.wait_ge(s["lo_ready"], pairs_done)
                hi = prob[:, j].bitcast(BF16).rearrange("p (n two) -> p n two", two=2)[:, :, 1]
                for a in range(2):
                    v = v_sb[:, bass.ds(step * 2 + (b * KT + a), 1), :].rearrange("p k c -> p (k c)")
                    for t in range(LT):
                        q = slice(a * N_BANK + t * P, a * N_BANK + (t + 1) * P)
                        for part, lhs in enumerate((hi[:, q], prob_lo[:, j, q])):
                            mm = nc.tensor.matmul(psum[:, 4 + slot, t * OC:(t + 1) * OC], lhs, v, start=False,
                                                  stop=(last_step and a == 1 and part == 1), skip_group_check=True)
                mm.then_inc(s["prob_slot_free"], 1)

            def unit(b, h, slot, nxt):
                u = h + b * H
                pe.wait_ge(s["out_slot_free"], u + 1)
                nc.tensor.matmul(psum[:, 4 + slot, 0:LT * OC], zeros[:], kparts[0:DH, 0:LT * OC], start=True, stop=False,
                                 skip_group_check=True)

                def round_of_steps(i, last_round):
                    for j in range(NP):
                        step = i * NP + j
                        count = u * STEPS + step
                        if not (last_round and j >= NP - LEAD):
                            scores(b, h, step + LEAD, j + LEAD, count + (LEAD + 1))
                        elif nxt is not None:
                            scores(nxt[0], nxt[1], j - (NP - LEAD), j + LEAD, count + (LEAD + 1))
                        values(b, step, j, u * (STEPS // 2) + i * (NP // 2) + (j // 2 + 1), slot, last_round and j == NP - 1)

                with pe.Fori(0, STEPS // NP - 1) as i:
                    round_of_steps(i, False)
                round_of_steps(STEPS // NP - 1, True)

            pe.wait_ge(consts_ready, CONSTS)
            for j in range(LEAD):
                scores(0, 0, j, j, j + 1)
            for b in range(B):
                with pe.Fori(0, H // 2 - 1) as pair:
                    unit(b, pair * 2, 0, (b, pair * 2 + 1))
                    unit(b, pair * 2 + 1, 1, (b, pair * 2 + 2))
                unit(b, H - 2, 0, (b, H - 1))
                unit(b, H - 1, 1, (b + 1, 0) if b + 1 < B else None)

            pe.wait_ge(s["wc_split"], 1)

            def concat(t):
                pe.wait_ge(s["concat_split"], t + 1)
                if t >= 2:
                    pe.wait_ge(s["concat_added"], t - 1)
                in_all, in_batch = slice(t * P, (t + 1) * P), slice((t % LT) * P, (t % LT + 1) * P)
                heads_of = (lambda c: feat_hi[:, c, in_all]), (lambda c: heads_lo[t // LT][:, c, in_batch])
                split_products(psum[:, 2 + t % 2, :], heads_of, parts(wc_hi, wc_lo, slice(0, D)), s["concat_mm"])

            for t in range(TT):
                pe.wait_ge(s["heads_ready"], t + 1)
                if t >= 2:
                    pe.wait_ge(s["concat_split"], t - 1)
                for c in range(DC):
                    last = nc.tensor.transpose(psum[:, t % 2, c * P:(c + 1) * P], heads[:, t, c * P:(c + 1) * P], ident[:])
                last.then_inc(s["concat_tp"], 1)
                if t:
                    concat(t - 1)
            concat(TT - 1)

            transpose_tokens(1, xn2)
            pe.wait_ge(s["wqkv_split"], 1)
            for i in range(2 * DC):
                b, m = divmod(i, DC)
                if m == 0:
                    pe.wait_ge(s["xT_split"], (b + 3) * DC)
                if i in (2, 3):
                    pe.wait_ge(s["xT_split"], 2 * DC + q_banks[i] + 1)
                if i >= 4:
                    pe.wait_ge(s["qkv_qdone"], i - 3)
                split_products(psum[:, q_banks[i % 4], :], parts(wqkv_hi[0], wqkv_lo[0], slice(m * P, (m + 1) * P)),
                               parts(feat_hi, feat_lo, slice(b * L, (b + 1) * L)), s["qkv_q"])
            pe.wait_ge(s["wqkv_split"], 3)
            for t in range(TT):
                rows = slice(t * P, (t + 1) * P)
                if t >= 2:
                    pe.wait_ge(s["qkv_kb"], t - 1)
                split_products(psum[:, 2 + t % 2, :], parts(feat_hi, feat_lo, rows), parts(wqkv_hi[1], wqkv_lo[1], slice(0, D)),
                               s["qkv_k"])
                if t >= 2:
                    pe.wait_ge(s["qkv_vdone"], t - 1)
                split_products(psum[:, 4 + t % 2, :], parts(feat_hi, feat_lo, rows), parts(wqkv_hi[2], wqkv_lo[2], slice(0, D)),
                               s["qkv_v"])
            pe.wait_ge(s["qkv_qdone"], 2 * DC)
            for i in range(2 * DC):
                b, c = divmod(i, DC)
                pe.wait_ge(s["qkv_kdone"], (b + 1) * LT)
                pe.wait_ge(s["qkv_vdone"], (b + 1) * LT)
                if i >= 2:
                    pe.wait_ge(s["state_done"], i - 1)
                for t in range(LT):
                    last = nc.tensor.matmul(psum[:, i % 2, 0:P + 1], kf[:, b * LT + t, c * P:(c + 1) * P],
                                            vf[:, b * LT + t, c, :], start=(t == 0), stop=(t == LT - 1))
                last.then_inc(s["state_mm"], 1)
            pe.wait_ge(s["state_done"], 2 * DC)
            for t in range(TT):
                if t >= 2:
                    pe.wait_ge(s["la_done"], t - 1)
                for c in range(DC):
                    last = nc.tensor.matmul(psum[:, 2 * (t % 2) + c // 2, (c % 2) * (P + 4):(c % 2 + 1) * (P + 4)],
                                            qf[:, c, t * P:(t + 1) * P], state[:, (t // LT) * DC + c, :],
                                            start=True, stop=True)
                last.then_inc(s["la_mm"], 1)

            pe.wait_ge(s["wproj_split"], 1)

            def project(t):
                pe.wait_ge(s["la_split"], t + 1)
                if t >= 2:
                    pe.wait_ge(s["proj_added"], t - 1)
                split_products(psum[:, 6 + t % 2, :], parts(feat_hi, feat_lo, slice(t * P, (t + 1) * P)),
                               parts(wproj_hi, wproj_lo, slice(0, D)), s["proj_mm"])

            for t in range(TT):
                pe.wait_ge(s["la_done"], t + 1)
                if t >= 2:
                    pe.wait_ge(s["la_split"], t - 1)
                for c in range(DC):
                    last = nc.tensor.transpose(psum[:, 4 + t % 2, c * P:(c + 1) * P], la[:, t, c * P:(c + 1) * P], ident[:])
                last.then_inc(s["la_tp"], 1)
                if t:
                    project(t - 1)
            project(TT - 1)

            transpose_tokens(2, xn2)
            pe.wait_ge(s["xT_split"], 6 * DC)
            pe.wait_ge(s["gate_split"], 1)
            for b in range(B):
                split_products(psum[0:E, 6 + b, :], parts(gate_hi, gate_lo, slice(0, E)),
                               parts(feat_hi, feat_lo, slice(b * L, (b + 1) * L)), s["logit_rows"])

            def transpose_logits():
                pe.wait_ge(s["logit_rows_copied"], B)
                for t in range(TT):
                    last = nc.tensor.transpose(psum[:, 7, t * E:(t + 1) * E], lg_rows[0:E, t // LT, (t % LT) * P:(t % LT + 1) * P],
                                               ident[0:E, 0:E])
                last.then_inc(s["logit_tp"], 1)

            def expert_out(i):
                e, b = divmod(i, B)
                if i == 0:
                    pe.wait_ge(s["logit_read"], 1)
                pe.wait_ge(s["ffn_s_split"], i + 1)
                half, k_half = divmod(e, E // 2)
                high, low = wo_hi[half][:, k_half, :], wo_lo[half][:, k_half, :]
                for t in range(LT):
                    k = i * LT + t
                    if k >= 4:
                        pe.wait_ge(s["ffn_added"], k - 3)
                    rows = slice(t * P, (t + 1) * P)
                    dst = psum[:, 4 + k % 4, :]
                    nc.tensor.matmul(dst, ffs_hi[:, i % 2, rows], high, start=True, stop=False)
                    nc.tensor.matmul(dst, ffs_hi[:, i % 2, rows], low, start=False, stop=False)
                    nc.tensor.matmul(dst, ffs_lo[:, i % 2, rows], high, start=False, stop=True).then_inc(s["ffn_y"], 1)

            for i in range(E * B):
                e, b = divmod(i, B)
                if i >= 2:
                    pe.wait_ge(s["ffn_s"], i - 1)
                half, k_half = divmod(e, E // 2)
                pe.wait_ge(s["ffnw_split"], e + 1)
                for bank, high, low, signal in ((0, wu_hi, wu_lo, s["ffn_u"]), (2, wv_hi, wv_lo, s["ffn_v"])):
                    split_products(psum[:, bank + i % 2, :], parts(high[half][:, k_half], low[half][:, k_half], slice(0, R)),
                                   parts(feat_hi, feat_lo, slice(b * L, (b + 1) * L)), signal)
                if i:
                    expert_out(i - 1)
                else:
                    transpose_logits()
            expert_out(E * B - 1)


_INS = ['x', 'ctx_1024', 'L0_xattn_w_q', 'L0_xattn_w_kv', 'L0_xattn_w_concat', 'L0_attn_w_qkv', 'L0_attn_b_qkv',
        'L0_attn_w_proj', 'L0_attn_b_proj', 'L0_ffn_gate_w', 'L0_ffn_Wu', 'L0_ffn_Wv', 'L0_ffn_Wo']
_OUTS = [((2, 512, 512), 'float32')]


def kernel(**inputs):
    import numpy as _np
    import concourse.bacc as _bacc
    from concourse import mybir as _mybir
    from concourse.bass_utils import run_bass_kernel_spmd as _run

    nc = _bacc.Bacc("TRN2", target_bir_lowering=False, num_devices=1)
    arrays, args = {}, []
    for name in _INS:
        a = _np.ascontiguousarray(inputs[name])
        arrays[f"in_{name}_dram"] = a
        args.append(nc.dram_tensor(f"in_{name}_dram", a.shape, _mybir.dt.from_np(a.dtype), kind="ExternalInput").ap())
    for i, (shape, dtype) in enumerate(_OUTS):
        dt = _mybir.dt.from_np(_np.dtype(dtype))
        args.append(nc.dram_tensor(f"out_{i}_dram", shape, dt, kind="ExternalOutput").ap())
    perceiver_block(nc, *args)
    r = _run(nc, [arrays], core_ids=[0])
    got = tuple(r.results[0][f"out_{i}_dram"] for i in range(len(_OUTS)))
    return got[0]
```
